# Optimizing a Trainium2 kernel written in Bass

```python
import numpy as np
import jax
import jax.numpy as jnp

def _softmax(x, axis=-1):
    return jax.nn.softmax(x, axis=axis)
def _gelu(x):
    return jax.nn.gelu(x, approximate=True)
def _silu(x):
    return jax.nn.silu(x)
def _sigmoid(x):
    return jax.nn.sigmoid(x)
def _layernorm(x, axis=-1, eps=1e-5):
    m = jnp.mean(x, axis=axis, keepdims=True)
    v = jnp.var(x, axis=axis, keepdims=True)
    return (x - m) / jnp.sqrt(v + eps)
def _scatter_add(tgt, idx, src, axis=0):
    return tgt.at[idx].add(src)
def _segment_sum(src, seg, n):
    return jax.ops.segment_sum(src, seg, n)

kernel_name = 'mk_metaformer_d1_conv_nhwc128_5a493d'

def setup_inputs(seed: int = 0):
    np.random.seed(seed)
    _w = jnp.asarray
    def _rec_inputs():
        import jax
        import jax.numpy as jnp
        _gk = jax.random.key(seed)
        x = -0.0003482 + 1 * jax.random.normal(jax.random.fold_in(_gk, 1), (1, 384, 384, 128), jnp.float32)
        return x
    x = _rec_inputs()
    def _L0_conv_setup():
        import jax, jax.numpy as jnp
        import numpy as np
        EPS = 1e-05

        def layer_norm(x, w, b):
            mu = jnp.mean(x, axis=-1, keepdims=True)
            var = jnp.mean(jnp.square(x - mu), axis=-1, keepdims=True)
            return (x - mu) * jax.lax.rsqrt(var + EPS) * w + b
        key = jax.random.key(seed)
        ks = jax.random.split(key, 12)
        B, N, D, H = (1, 384, 128, 128)
        s = 1.0 / np.sqrt(D)
        so = 1.0 / np.sqrt(H)
        return {'x': jax.random.normal(ks[0], (B, N, N, D), dtype=jnp.float32), 'mask': jax.random.uniform(ks[1], (B, N, N), dtype=jnp.float32), 'norm_w': jnp.ones((D,), jnp.float32), 'norm_b': jnp.zeros((D,), jnp.float32), 'W_left': jax.random.normal(ks[2], (H, D), jnp.float32) * s, 'W_right': jax.random.normal(ks[3], (H, D), jnp.float32) * s, 'W_left_gate': jax.random.normal(ks[4], (H, D), jnp.float32) * s, 'W_right_gate': jax.random.normal(ks[5], (H, D), jnp.float32) * s, 'W_out_gate': jax.random.normal(ks[6], (H, D), jnp.float32) * s, 'out_norm_w': jnp.ones((H,), jnp.float32), 'out_norm_b': jnp.zeros((H,), jnp.float32), 'W_out': jax.random.normal(ks[7], (D, H), jnp.float32) * so}
    _L0_conv_all = _L0_conv_setup()
    _L0_conv_in = {k: v for k, v in _L0_conv_all.items() if k in ('mask', 'norm_w', 'norm_b', 'W_left', 'W_right', 'W_left_gate', 'W_right_gate', 'W_out_gate', 'out_norm_w', 'out_norm_b', 'W_out', )}
    del _L0_conv_all

    def _L0_ffn_setup():
        import jax, jax.numpy as jnp
        import numpy as np
        B, S, D, E, H, O, K = (512, 2048, 128, 64, 512, 128, 8)
        key = jax.random.key(seed)
        k0, k1, k2, k3 = jax.random.split(key, 4)
        x = jax.random.normal(k0, (B, S, D), dtype=jnp.float32)
        gate_w = jax.random.normal(k1, (E, D), dtype=jnp.float32) * (1.0 / np.sqrt(D))
        gate_b = jnp.zeros((E,), dtype=jnp.float32)
        weight1 = jax.random.uniform(k2, (E, D + 1, H), dtype=jnp.float32, minval=-1.0, maxval=1.0) * (1.0 / np.sqrt(D + 1))
        weight2 = jax.random.uniform(k3, (E, H + 1, O), dtype=jnp.float32, minval=-1.0, maxval=1.0) * (1.0 / np.sqrt(H + 1))
        return {'x': x, 'gate_w': gate_w, 'gate_b': gate_b, 'weight1': weight1, 'weight2': weight2}
    _L0_ffn_all = _L0_ffn_setup()
    _L0_ffn_in = {k: v for k, v in _L0_ffn_all.items() if k in ('gate_w', 'gate_b', 'weight1', 'weight2', )}
    del _L0_ffn_all

    return {
        "x": x,
        "L0_conv_mask": _L0_conv_in["mask"],
        "L0_conv_norm_w": _L0_conv_in["norm_w"],
        "L0_conv_norm_b": _L0_conv_in["norm_b"],
        "L0_conv_W_left": _L0_conv_in["W_left"],
        "L0_conv_W_right": _L0_conv_in["W_right"],
        "L0_conv_W_left_gate": _L0_conv_in["W_left_gate"],
        "L0_conv_W_right_gate": _L0_conv_in["W_right_gate"],
        "L0_conv_W_out_gate": _L0_conv_in["W_out_gate"],
        "L0_conv_out_norm_w": _L0_conv_in["out_norm_w"],
        "L0_conv_out_norm_b": _L0_conv_in["out_norm_b"],
        "L0_conv_W_out": _L0_conv_in["W_out"],
        "L0_ffn_gate_w": _L0_ffn_in["gate_w"],
        "L0_ffn_gate_b": _L0_ffn_in["gate_b"],
        "L0_ffn_weight1": _L0_ffn_in["weight1"],
        "L0_ffn_weight2": _L0_ffn_in["weight2"],
    }

def reference(x, L0_conv_mask, L0_conv_norm_w, L0_conv_norm_b, L0_conv_W_left, L0_conv_W_right, L0_conv_W_left_gate, L0_conv_W_right_gate, L0_conv_W_out_gate, L0_conv_out_norm_w, L0_conv_out_norm_b, L0_conv_W_out, L0_ffn_gate_w, L0_ffn_gate_b, L0_ffn_weight1, L0_ffn_weight2):
    import jax
    import jax.numpy as jnp
    def _L0_conv_ref(x, mask, norm_w, norm_b, W_left, W_right, W_left_gate, W_right_gate, W_out_gate, out_norm_w, out_norm_b, W_out):
        import jax, jax.numpy as jnp
        import numpy as np
        EPS = 1e-05

        def layer_norm(x, w, b):
            mu = jnp.mean(x, axis=-1, keepdims=True)
            var = jnp.mean(jnp.square(x - mu), axis=-1, keepdims=True)
            return (x - mu) * jax.lax.rsqrt(var + EPS) * w + b
        x = layer_norm(x, norm_w, norm_b).astype(jnp.float32)
        left = x @ W_left.T
        right = x @ W_right.T
        left_gate = jax.nn.sigmoid(x @ W_left_gate.T)
        right_gate = jax.nn.sigmoid(x @ W_right_gate.T)
        out_gate = jax.nn.sigmoid(x @ W_out_gate.T)
        m = mask[..., None]
        left = left * m * left_gate
        right = right * m * right_gate
        out = jnp.einsum('bikd,bjkd->bijd', left.astype(jnp.bfloat16), right.astype(jnp.bfloat16))
        out = layer_norm(out.astype(jnp.float32), out_norm_w, out_norm_b) * out_gate
        return out @ W_out.T

    def _L0_ffn_ref(x, gate_w, gate_b, weight1, weight2):
        import jax, jax.numpy as jnp
        import numpy as np
        B, S, D, E, H, O, K = (512, 2048, 128, 64, 512, 128, 8)
        Bn, Sn, Dn = x.shape
        logits = jnp.einsum('bsd,ed->bse', x, gate_w) + gate_b
        probs = jax.nn.softmax(logits, axis=1)
        vals, idx = jax.lax.top_k(probs.transpose(0, 2, 1), K)
        topv = vals.transpose(0, 2, 1)
        topi = idx.transpose(0, 2, 1)
        flat_idx = topi.reshape(Bn, K * E)
        gathered = jnp.take_along_axis(x, flat_idx[:, :, None], axis=1)
        gathered = gathered.reshape(Bn, K, E, Dn)
        pooled = jnp.einsum('bked,bke->bed', gathered, topv)
        ones = jnp.ones((E, Bn, 1), dtype=x.dtype)
        h = jnp.concatenate([pooled.transpose(1, 0, 2), ones], axis=-1)
        h = jax.nn.gelu(jnp.einsum('ebd,edh->ebh', h, weight1), approximate=False)
        h = jnp.concatenate([h, ones], axis=-1)
        out = jnp.einsum('ebh,eho->ebo', h, weight2)
        out = out.transpose(1, 0, 2)
        weighted = jnp.einsum('beo,bke->bkeo', out, topv).reshape(Bn, K * E, O)
        outputs = jnp.zeros((Bn, Sn, O), dtype=x.dtype)
        outputs = outputs.at[jnp.arange(Bn)[:, None], flat_idx].add(weighted)
        return outputs

    def _gn(v, G=32, eps=1e-5):
        B_, H_, W_, C_ = v.shape
        g = v.reshape(B_, H_, W_, G, C_ // G)
        m = jnp.mean(g, axis=(1, 2, 4), keepdims=True)
        s = jnp.var(g, axis=(1, 2, 4), keepdims=True)
        return ((g - m) / jnp.sqrt(s + eps)).reshape(v.shape)

    def _ln_c(v, eps=1e-6):
        m = jnp.mean(v, axis=-1, keepdims=True)
        s = jnp.var(v, axis=-1, keepdims=True)
        return (v - m) / jnp.sqrt(s + eps)

    def _ln_t(v, eps=1e-5):
        m = jnp.mean(v, axis=-1, keepdims=True)
        s = jnp.var(v, axis=-1, keepdims=True)
        return (v - m) / jnp.sqrt(s + eps)

    def _to_tokens(v):
        B_, H_, W_, C_ = v.shape
        return v.reshape(B_, H_ * W_, C_)
    def _from_tokens(t, like):
        return t.reshape(like.shape)

    x = x + _L0_conv_ref(_ln_c(x), L0_conv_mask, L0_conv_norm_w, L0_conv_norm_b, L0_conv_W_left, L0_conv_W_right, L0_conv_W_left_gate, L0_conv_W_right_gate, L0_conv_W_out_gate, L0_conv_out_norm_w, L0_conv_out_norm_b, L0_conv_W_out)
    t = _to_tokens(x)
    t = t + _L0_ffn_ref(_ln_t(t), L0_ffn_gate_w, L0_ffn_gate_b, L0_ffn_weight1, L0_ffn_weight2)
    x = _from_tokens(t, x)
    return x


_drawn_inputs = setup_inputs


def setup_inputs(seed=0):
    import zlib

    import numpy as np

    out = dict(_drawn_inputs(seed))
    spreads = {'L0_conv_norm_w': (1.0, 0.2),
     'L0_conv_norm_b': (0.0, 0.1),
     'L0_conv_out_norm_w': (1.0, 0.2),
     'L0_conv_out_norm_b': (0.0, 0.1),
     'L0_ffn_gate_b': (0.0, 0.1)}
    factors = {'L0_ffn_gate_w': 8.0, 'L0_ffn_weight1': 8.0, 'L0_ffn_weight2': 8.0}
    for name, (base, spread) in spreads.items():
        noise = np.random.default_rng([zlib.crc32(name.encode()), seed]).standard_normal(out[name].shape)
        drawn = base * np.exp(spread * noise) if base else spread * noise
        out[name] = jnp.asarray(drawn.astype(out[name].dtype))
    for name, factor in factors.items():
        out[name] = (out[name] * factor).astype(out[name].dtype)
    return out
```

```python
import concourse.bass as bass
from concourse import mybir
from contextlib import ExitStack


def metaformer_layer_kernel(
    nc: bass.Bass,
    x: bass.AP,
    mask: bass.AP,
    norm_w: bass.AP,
    norm_b: bass.AP,
    W_left: bass.AP,
    W_right: bass.AP,
    W_left_gate: bass.AP,
    W_right_gate: bass.AP,
    W_out_gate: bass.AP,
    out_norm_w: bass.AP,
    out_norm_b: bass.AP,
    W_out: bass.AP,
    gate_w: bass.AP,
    gate_b: bass.AP,
    weight1: bass.AP,
    weight2: bass.AP,
    out: bass.AP,
):
    fp32 = mybir.dt.float32
    bf16 = mybir.dt.bfloat16
    u32 = mybir.dt.uint32
    i32 = mybir.dt.int32
    ALU = mybir.AluOpType
    ACT = mybir.ActivationFunctionType
    AX = mybir.AxisListType
    ds = bass.ds

    P = 128
    N = x.shape[1]
    D = x.shape[3]
    E = gate_w.shape[0]
    HF = weight1.shape[2]
    K = 8
    S = N * N
    NBLK = N // P
    TB = 8
    TU = TB // 2
    RB = N // TB
    NB = NBLK * RB
    CB = P // TB
    NCH = NB // CB
    EPS_C = 1e-6
    EPS = 1e-5
    HC = HF // P
    XG = 8
    NXG = E // XG

    x3 = x[0]
    mask2 = mask[0]
    out3 = out[0]
    rows = out[0].rearrange("i j d -> (i j) d")

    ctx = ExitStack()
    with ctx:
        def sb(name, shape, dt):
            return ctx.enter_context(nc.sbuf_tensor(name, shape, dt))

        def pb(name, shape, dt):
            return ctx.enter_context(nc.psum_tensor(name, shape, dt))

        def sem(name):
            return ctx.enter_context(nc.semaphore(name))

        sides = nc.dram_tensor("sides", (2, NBLK, NBLK, P, D * P), bf16, kind="Internal").ap()

        arena = sb("arena", [P, 4 * D * P], bf16)
        stage = arena[:, :].rearrange("k (c s d i) -> k c s d i", c=2, s=2, d=D)
        right_res = arena[:, 0:2 * D * P].rearrange("k (t d j) -> k t d j", t=2, d=D)
        tri = arena[:, 2 * D * P:4 * D * P].rearrange("j (c i d) -> j c i d", c=2, i=P)
        wbuf = arena[:, 0:2 * D * P].bitcast(fp32)
        w1buf = wbuf[:, 0:2 * XG * HF].rearrange("p (s e h) -> p s e h", s=2, e=XG)
        w2buf = wbuf[:, 2 * XG * HF:4 * XG * HF].rearrange("p (s e h) -> p s e h", s=2, e=XG)
        tail = arena[:, 2 * D * P:4 * D * P]
        used = [0]

        def carve(shape, dt=fp32):
            n = 1
            for v in shape:
                n *= v
            at = used[0]
            used[0] += 2 * n
            assert used[0] <= 2 * D * P
            flat = tail[:, at:at + 2 * n].bitcast(dt)
            if len(shape) == 2:
                return flat.rearrange("p (a b) -> p a b", a=shape[0])
            return flat

        iota_i, iota_f, pick = carve([NB * K], i32), carve([NB * K]), carve([NB * K])
        ones, earlier = carve([4 * 4 * P]), carve([4, 4 * P])
        idx_row, share, part, diag = (carve([K * E]) for _ in range(4))
        t_rows, u_rows, new_rows = (carve([4, D]) for _ in range(3))
        dtop, id2 = carve([4, E]), carve([E])
        b1_t, b2_t, pooled_t = carve([HC * E]), carve([E]), carve([E])
        hid, hpre = carve([2, HC * XG]), carve([2, HC * XG])
        out_t, out_e = carve([E]), carve([D])
        wexp = carve([NB])
        both, kv, sel = carve([2, 18]), carve([2, K]), carve([2, 4])
        v16, t16 = carve([2, K]), carve([2, K])
        pos_i, raw_i, bi, qi = (carve([K], u32) for _ in range(4))
        pos_f, raw, bf, qf, tok, v8, ev = (carve([K]) for _ in range(7))
        idx_i, idx_w = carve([4], i32), carve([4], i32)
        mv4, rst4, dup = carve([4, 2]), carve([4]), carve([4])
        hm, den = carve([2]), carve([1])
        par384, negtop, neg2 = carve([1]), carve([1]), carve([1])
        V_TOP, V_FIN, V_M2, V_KV, V_DIAG, V_IDX = 5, 31, 35, 49, 50, 53
        V_VAR, V_U, V_PT, V_OT, V_OE, V_NEW = 83, 84, 90, 97, 98, 99

        ring = sb("ring", [P, 2 * 4 * TB * P], bf16)
        lr = ring[:, :].rearrange("k (s q d i) -> k s q d i", s=2, q=4, d=TB)
        ring32 = ring[:, :].bitcast(fp32)
        mask_t = ring32[:, 0:NBLK * N].rearrange("k (b i) -> k b i", b=NBLK)

        xin = sb("xin", [P, 2, TB, D], fp32)
        tout = sb("tout", [P, 2, TB, D], fp32)
        sig = tout[:, 0, :, :].rearrange("p (j t) d -> p j (t d)", j=2).rearrange(
            "p j (t c) -> p j t c", t=2)
        xh = sb("xh", [P, 2, TU * D], fp32)
        xnt = sb("xnt", [D, 2, TU * P], fp32)
        on = sb("on", [P, 2, TU * D], fp32)
        gated = sb("gated", [D, 2, TU * P], fp32)
        tt = sb("tt", [D, 2, TU * P], fp32)
        w_lr = tt[:, 0, :]
        lgs = sb("lgs", [P, 2, TU * E], fp32)
        stats = sb("stats", [P, 2, NB * TB], fp32)
        cand = sb("cand", [P, NB, K], fp32)
        cidx = sb("cidx", [P, NB, K], fp32)
        csum = sb("csum", [P, NB], fp32)
        ident = sb("ident", [P, P], fp32)
        w_og = sb("w_og", [D, D], fp32)
        w_o = sb("w_o", [D, D], fp32)
        g_c = sb("g_c", [D, E], fp32)
        cols = sb("cols", [P, 4], fp32)
        gb = sb("gb", [P, 1], fp32)
        mhalf = sb("mhalf", [P, TB], fp32)
        bst = sb("bst", [P, TB, 6], fp32)
        tmp = sb("tmp", [P, 3, TB], fp32)
        sm = sb("sm", [P, 2, 2, TB], fp32)
        xst = sb("xst", [P, 2, 2, TB], fp32)
        smt = sb("smt", [P, 2, TB], fp32)
        tst = sb("tst", [P, 2, TB], fp32)
        smo = sb("smo", [P, 2, TB], fp32)
        ost = sb("ost", [P, 2, TB], fp32)
        m8 = sb("m8", [P, K], fp32)
        negm = sb("negm", [P, 1], fp32)
        i8 = sb("i8", [P, K], u32)
        esum = sb("esum", [P, 1], fp32)
        ejunk = sb("ejunk", [P, TB * E], bf16)
        wraw = xin[:, 0, :, :]

        bank = [pb(f"bank{i}", [P, 512], fp32) for i in range(8)]

        s_ident = sem("s_ident")
        s_const = sem("s_const")
        s_pool = sem("s_pool")
        s_dve = sem("s_dve")
        s_wload = sem("s_wload")
        s_wt = sem("s_wt")
        s_wcopy = sem("s_wcopy")
        s_gmean = sem("s_gmean")
        s_gcen = sem("s_gcen")
        a_x = [sem(f"a_x{i}") for i in range(2)]
        a_bn = sem("a_bn")
        a_s1 = sem("a_s1")
        a_s2 = sem("a_s2")
        a_sm = sem("a_sm")
        a_arg = sem("a_arg")
        a_pow = sem("a_pow")
        a_keep = sem("a_keep")
        a_xh = sem("a_xh")
        a_tp = sem("a_tp")
        a_xn = sem("a_xn")
        a_lr = sem("a_lr")
        a_sig = sem("a_sig")
        a_side = sem("a_side")
        a_store = sem("a_store")
        b_x = [sem(f"b_x{i}") for i in range(2)]
        b_lr = [sem(f"b_lr{i}") for i in range(2)]
        b_res = [sem(f"b_res{i}") for i in range(2)]
        b_store = [sem(f"b_store{i}") for i in range(2)]
        b_xst = sem("b_xst")
        b_xh = sem("b_xh")
        b_xtp = sem("b_xtp")
        b_xn = sem("b_xn")
        b_gate = sem("b_gate")
        b_tanh = sem("b_tanh")
        b_tri = sem("b_tri")
        b_triout = sem("b_triout")
        b_bno = sem("b_bno")
        b_o1 = sem("b_o1")
        b_o2 = sem("b_o2")
        b_smo = sem("b_smo")
        b_oarg = sem("b_oarg")
        b_ost = sem("b_ost")
        b_on = sem("b_on")
        b_otp = sem("b_otp")
        b_onw = sem("b_onw")
        b_gated = sem("b_gated")
        b_y = sem("b_y")
        b_t = sem("b_t")
        b_bnt = sem("b_bnt")
        b_t1 = sem("b_t1")
        b_t2 = sem("b_t2")
        b_smt = sem("b_smt")
        b_targ = sem("b_targ")
        b_rst = sem("b_rst")
        b_ttp = sem("b_ttp")
        b_tt = sem("b_tt")
        b_logit = sem("b_logit")
        b_lgs = sem("b_lgs")
        b_ltp = sem("b_ltp")
        b_m8 = sem("b_m8")
        b_negm = sem("b_negm")
        b_i8 = sem("b_i8")
        b_keep = sem("b_keep")
        b_exp = sem("b_exp")
        b_expsum = sem("b_expsum")
        c_w1 = [sem(f"c_w1{i}") for i in range(2)]
        c_w2 = [sem(f"c_w2{i}") for i in range(2)]
        c_bias = sem("c_bias")
        c_iota = sem("c_iota")
        c_v = sem("c_v")
        c_act = sem("c_act")
        c_half = sem("c_half")
        c_kv = sem("c_kv")
        c_pool = sem("c_pool")
        c_row = sem("c_row")
        c_gather = sem("c_gather")
        c_btp = sem("c_btp")
        c_pooled = sem("c_pooled")
        c_h = sem("c_h")
        c_hb = sem("c_hb")
        c_gelu = sem("c_gelu")
        c_o = sem("c_o")
        c_otp = sem("c_otp")
        c_delta = sem("c_delta")
        c_scatter = sem("c_scatter")

        def live(n):
            return not isinstance(n, int) or 0 <= n < NB

        def await_(eng, s, v):
            if not isinstance(v, int) or v > 0:
                eng.wait_ge(s, v)

        def pass_on(eng, s):
            eng.sem_inc(s, 1)

        def rows_of(b):
            return ds((b % RB) * TB, TB)

        def cols_of(b):
            return ds((b // RB) * P, P)

        block = ctx.enter_context(nc.Block())

        @block.sync
        def _(sp):
            for n, w in enumerate([W_left, W_right, W_left_gate, W_right_gate, W_out_gate, W_out]):
                sp.dma_start(wraw[:, n, :], w).then_inc(s_wload, 16)
            sp.dma_start(wraw[0:E, 6, :], gate_w).then_inc(s_wload, 16)
            for n, w in enumerate([norm_w, norm_b, out_norm_w, out_norm_b]):
                sp.dma_start(cols[:, n:n + 1], w.rearrange("(d o) -> d o", o=1)).then_inc(s_wload, 16)
            for h in range(2):
                sp.dma_start(gb[h * E:(h + 1) * E, :], gate_b.rearrange("(d o) -> d o", o=1)).then_inc(s_wload, 16)
            sp.dma_start(tout[:, :, :, :].rearrange("p s t d -> p (s t d)")[:, 0:NBLK * N].rearrange(
                "p (b k) -> p b k", b=NBLK), mask2.rearrange("(b i) k -> i b k", b=NBLK)).then_inc(s_wload, 16)

            def load_x(b, par):
                await_(sp, a_xh, 2 * (b - 2) + 2)
                sp.dma_start(xin[:, par, :, :], x3[rows_of(b), cols_of(b), :].rearrange("i j d -> j i d")
                             ).then_inc(a_x[par], 16)

            sp.wait_ge(s_wcopy, 17)
            load_x(0, 0)
            load_x(1, 1)
            for c in range(NCH):
                last = NB if c == NCH - 1 else CB * (c + 1) + 2
                with sp.Fori((CB * c + 2) // 2, (last) // 2) as b_2:
                    b = 2 * b_2
                    load_x(b, 0)
                    load_x(b + 1, 1)
                sp.wait_ge(a_side, P * (c + 1))
                for side in range(2):
                    sp.dma_start(sides[side, c // NBLK, c % NBLK],
                                 stage[:, c % 2, side, :, :].rearrange("k d i -> k (d i)")).then_inc(a_store, 16)
            sp.wait_ge(a_store, 32 * NCH)

            def load_lr(eb, par, resident):
                c = eb // CB
                jb, ib = c // NBLK, c % NBLK
                at = (eb % CB) * TB * P
                await_(sp, b_tri, 2 * (eb - 2) + 2)
                sp.dma_start(lr[:, par, 0:3, :, :].rearrange("k q d i -> k q (d i)"),
                             sides[0, :, ds(ib, 1), :, ds(at, TB * P)].rearrange("t o k n -> k (t o) n")
                             ).then_inc(b_lr[par], 16)
                sp.dma_start(lr[:, par, 3, :, :].rearrange("k d i -> k (d i)"),
                             sides[1, 2, ds(jb, 1), :, ds(at, TB * P)].rearrange("o k n -> k (o n)")
                             ).then_inc(b_lr[par], 16)
                if resident:
                    sp.dma_start(right_res[:, :, ds((eb % CB) * TB, TB), :].rearrange("k t d j -> k t (d j)"),
                                 sides[1, 0:2, ds(jb, 1), :, ds(at, TB * P)].rearrange("t o k n -> k (t o) n")
                                 ).then_inc(b_res[par], 16)

            def load_x2(b, par):
                await_(sp, b_t, 2 * (b - 2) + 2)
                await_(sp, b_xh, 2 * (b - 2) + 2)
                sp.dma_start(xin[:, par, :, :], x3[rows_of(b), cols_of(b), :].rearrange("i j d -> j i d")
                             ).then_inc(b_x[par], 16)

            def store_t(b, par):
                sp.wait_ge(b_t, 2 * b + 2)
                sp.dma_start(out3[rows_of(b), cols_of(b), :].rearrange("i j d -> j i d"), tout[:, par, :, :]
                             ).then_inc(b_store[par], 16)

            load_lr(0, 0, True)
            load_lr(1, 1, True)
            load_x2(0, 0)
            load_x2(1, 1)
            with sp.Fori(1, (CB) // 2) as eb_2:
                eb = 2 * eb_2
                load_lr(eb, 0, True)
                load_lr(eb + 1, 1, True)
            load_lr(CB, 0, False)
            load_lr(CB + 1, 1, False)
            LA = CB + 2
            for lo, hi, resident in [(0, 30, False), (30, 46, True), (46, 78, False), (78, 94, True),
                                     (94, NB - LA, False)]:
                with sp.Fori(lo // 2, (hi) // 2) as b_2:
                    b = 2 * b_2
                    for par in range(2):
                        load_lr(b + par + LA, par, resident)
                        store_t(b + par, par)
                        load_x2(b + par + 2, par)
            with sp.Fori((NB - LA) // 2, (NB - 2) // 2) as b_2:
                b = 2 * b_2
                for par in range(2):
                    store_t(b + par, par)
                    load_x2(b + par + 2, par)
            sp.wait_ge(b_tri, 2 * NB)

            def load_experts(n, par):
                sp.dma_start(w1buf[:, par, :, :], weight1[ds(n * XG, XG), 0:D, :].rearrange("e d h -> d e h")
                             ).then_inc(c_w1[par], 16)
                for e in range(XG):
                    sp.dma_start(w2buf[:, par, e, :].rearrange("p (c o) -> p c o", c=HC),
                                 weight2[ds(n * XG + e, 1), 0:HF, :].rearrange("a (c h) o -> h (a c) o", c=HC)
                                 ).then_inc(c_w2[par], 16)

            load_experts(0, 0)
            load_experts(1, 1)
            store_t(NB - 2, 0)
            store_t(NB - 1, 1)
            sp.dma_start(ring32[0:E, 0:HF], weight1[:, D, :]).then_inc(c_bias, 16)
            sp.dma_start(ring32[0:E, HF:HF + D], weight2[:, HF, :]).then_inc(c_bias, 16)
            sp.wait_ge(c_v, V_FIN)
            sp.dma_start(both[0:E, 1, :], both[E:2 * E, 0, :]).then_inc(c_half, 16)
            sp.wait_ge(c_v, V_KV)
            sp.dma_start(kv[E:2 * E, :, :], kv[0:E, :, :]).then_inc(c_kv, 16)
            with sp.Fori(1, (NXG) // 2) as n_2:
                n = 2 * n_2
                for par in range(2):
                    sp.wait_ge(c_o, n + par - 1)
                    load_experts(n + par, par)
            sp.wait_ge(c_scatter, 64)

        @block.gpsimd
        def _(pool):
            nc.gpsimd.memset(ident[:, :], 0.0).then_inc(s_ident, 1)
            nc.gpsimd.memset(mhalf[:, :], -0.5).then_inc(s_const, 1)
            pool.wait_ge(s_ident, 1)
            nc.gpsimd.affine_select(out=ident[:, :], in_=ident[:, :], compare_op=ALU.not_equal, fill=1.0,
                                    base=0, pattern=[[-1, P]], channel_multiplier=1).then_inc(s_ident, 1)

            def norm_x(b, par):
                pool.wait_ge(a_sm, b + 1)
                await_(pool, a_keep, b - 1)
                pass_on(pool, s_pool)
                nc.gpsimd.tensor_scalar(xst[:, par, 1, :], sm[:, par, 1, :], (1.0 + EPS) / D, EPS * EPS_C,
                                        ALU.mult, ALU.add).then_inc(a_arg, 1)
                nc.gpsimd.tensor_scalar(xst[:, par, 0, :], sm[:, par, 0, :], -0.5, 0.0,
                                        ALU.mult, ALU.add)
                pool.wait_ge(a_arg, b + 1)
                nc.gpsimd.tensor_tensor(xst[:, par, 1, :], xst[:, par, 1, :], mhalf[:, :], ALU.pow
                                        ).then_inc(a_pow, 1)
                pool.wait_ge(a_pow, b + 1)
                nc.gpsimd.tensor_copy(stats[:, :, ds(b * TB, TB)], xst[:, par, :, :]).then_inc(a_keep, 1)
                for h in range(2):
                    await_(pool, a_tp, 2 * (b - 1) + h + 1)
                    pass_on(pool, s_pool)
                    for t in range(TU):
                        n = h * TU + t
                        last = nc.gpsimd.tensor_scalar(xh[:, h, t * D:(t + 1) * D], xin[:, par, n, :],
                                                       xst[:, par, 0, n:n + 1], xst[:, par, 1, n:n + 1],
                                                       ALU.add, ALU.mult)
                    last.then_inc(a_xh, 1)

            pool.wait_ge(s_const, 1)
            norm_x(0, 0)
            norm_x(1, 1)
            with pool.Fori(1, (NB) // 2) as b_2:
                b = 2 * b_2
                norm_x(b, 0)
                norm_x(b + 1, 1)

            pool.wait_ge(a_keep, NB)

            def norm_x2(b, par):
                nc.gpsimd.tensor_copy(xst[:, par, :, :], stats[:, :, ds(b * TB, TB)]).then_inc(b_xst, 1)
                pool.wait_ge(b_x[par], 16 * (b // 2) + 16)
                pool.wait_ge(b_xst, b + 1)
                for h in range(2):
                    if isinstance(b, int) and b == 0:
                        pool.wait_ge(a_tp, 2 * NB - 1 + h)
                    else:
                        pool.wait_ge(b_xtp, 2 * (b - 1) + h + 1)
                    pass_on(pool, s_pool)
                    for t in range(TU):
                        n = h * TU + t
                        last = nc.gpsimd.tensor_scalar(xh[:, h, t * D:(t + 1) * D], xin[:, par, n, :],
                                                       xst[:, par, 0, n:n + 1], xst[:, par, 1, n:n + 1],
                                                       ALU.add, ALU.mult)
                    last.then_inc(b_xh, 1)

            def stats_t(b):
                pool.wait_ge(b_smt, b + 1)
                await_(pool, b_lgs, 2 * b)
                pass_on(pool, s_pool)
                nc.gpsimd.tensor_scalar(tst[:, 1, :], smt[:, 1, :], 1.0 / D, EPS, ALU.mult, ALU.add
                                        ).then_inc(b_targ, 1)
                pool.wait_ge(b_targ, b + 1)
                nc.gpsimd.tensor_tensor(tst[:, 1, :], tst[:, 1, :], mhalf[:, :], ALU.pow).then_inc(b_rst, 1)

            def stats_o(b):
                pool.wait_ge(b_smo, b + 1)
                await_(pool, b_on, 2 * b)
                pass_on(pool, s_pool)
                nc.gpsimd.tensor_scalar(ost[:, 1, :], smo[:, 1, :], 1.0 / D, EPS, ALU.mult, ALU.add
                                        ).then_inc(b_oarg, 1)
                nc.gpsimd.tensor_scalar(ost[:, 0, :], smo[:, 0, :], -0.5, 0.0, ALU.mult, ALU.add)
                pool.wait_ge(b_oarg, b + 1)
                nc.gpsimd.tensor_tensor(ost[:, 1, :], ost[:, 1, :], mhalf[:, :], ALU.pow).then_inc(b_ost, 1)

            def step(b, par):
                if live(b - 1):
                    stats_t(b - 1)
                if live(b + 1):
                    stats_o(b + 1)
                    norm_x2(b + 1, 1 - par)

            norm_x2(0, 0)
            stats_o(0)
            step(0, 0)
            step(1, 1)
            with pool.Fori(1, (NB - 2) // 2) as b_2:
                b = 2 * b_2
                step(b, 0)
                step(b + 1, 1)
            for b in range(NB - 2, NB + 1):
                step(b, b % 2)

            pool.wait_ge(b_on, 2 * NB)
            nc.gpsimd.iota(iota_i, [[1, NB * K]], base=0, channel_multiplier=0).then_inc(c_iota, 1)
            nc.gpsimd.memset(ones[:, :], 1.0).then_inc(c_iota, 1)
            pool.wait_ge(c_iota, 2)
            nc.gpsimd.affine_select(out=earlier, in_=ones[:, :].rearrange("p (s a) -> p s a", s=4),
                                    compare_op=ALU.is_gt, fill=0.0, base=0,
                                    pattern=[[P, 4], [-1, 4 * P]], channel_multiplier=1).then_inc(c_iota, 1)
            pool.wait_ge(c_v, V_IDX)
            for par in range(2):
                pool.wait_ge(b_store[par], 16 * NB // 2)
            for s in range(4):
                pool.indirect_dma_start(
                    out=t_rows[:, s, :], out_offset=None, in_=rows,
                    in_offset=bass.IndirectOffsetOnAxis(ap=idx_i[:, s:s + 1], axis=0)).then_inc(c_gather, 16)
            pool.wait_ge(c_v, V_VAR)
            nc.gpsimd.tensor_scalar(rst4[:, :], mv4[:, :, 1], 1.0, EPS, ALU.mult, ALU.add).then_inc(c_pool, 1)
            pool.wait_ge(c_pool, 1)
            nc.gpsimd.tensor_tensor(rst4[:, :], rst4[:, :], mhalf[:, 0:4], ALU.pow).then_inc(c_pool, 1)
            pool.wait_ge(c_v, V_NEW)
            for s in range(4):
                pool.indirect_dma_start(
                    out=rows, out_offset=bass.IndirectOffsetOnAxis(ap=idx_w[:, s:s + 1], axis=0),
                    in_=new_rows[:, s, :], in_offset=None, bounds_check=S - 1, oob_is_err=False
                ).then_inc(c_scatter, 16)
            pool.wait_ge(c_scatter, 64)

        @block.tensor
        def _(pe):
            pe.wait_ge(s_ident, 2)
            pe.wait_ge(s_wload, 16 * 14)
            for n in range(6):
                if n >= 2:
                    pe.wait_ge(s_wcopy, n - 1)
                nc.tensor.transpose(bank[n % 2][:, 0:P], wraw[:, n, :], ident[:, :]).then_inc(s_wt, 1)
            mrow = tout[:, :, :, :].rearrange("p s t d -> p (s t d)")[:, 0:NBLK * N].rearrange(
                "p (b k) -> p b k", b=NBLK)
            for n in range(NBLK * NBLK):
                pe.wait_ge(s_wcopy, n + 5)
                nc.tensor.transpose(bank[n % 2][:, 0:P], mrow[:, n // NBLK, (n % NBLK) * P:(n % NBLK + 1) * P],
                                    ident[:, :]).then_inc(s_wt, 1)
            pe.wait_ge(s_wcopy, 15)
            pe.wait_ge(s_gcen, 1)
            nc.tensor.transpose(bank[1][:, 0:E], wraw[0:E, 7, :], ident[0:E, 0:E]).then_inc(s_wt, 1)

            def transpose_x(u, h):
                pe.wait_ge(a_xh, u + 1)
                await_(pe, a_xn, u - 1)
                for t in range(TU):
                    last = nc.tensor.transpose(bank[h][:, t * P:(t + 1) * P], xh[:, h, t * D:(t + 1) * D],
                                               ident[:, :])
                last.then_inc(a_tp, 1)

            def project(u, h):
                pe.wait_ge(a_xn, u + 1)
                for t in range(TU):
                    await_(pe, a_side, 4 * (u - 1) + t + 1)
                    nc.tensor.matmul(bank[2 + t][:, :], xnt[:, h, t * P:(t + 1) * P], w_lr,
                                     start=True, stop=True).then_inc(a_lr, 1)

            pe.wait_ge(s_wcopy, 17)
            transpose_x(0, 0)
            for b in range(2):
                transpose_x(2 * b + 1, 1)
                project(2 * b, 0)
                transpose_x(2 * b + 2, 0)
                project(2 * b + 1, 1)
            with pe.Fori(2, NB - 1, 1) as b:
                transpose_x(2 * b + 1, 1)
                project(2 * b, 0)
                transpose_x(2 * b + 2, 0)
                project(2 * b + 1, 1)
            transpose_x(2 * NB - 1, 1)
            project(2 * NB - 2, 0)
            project(2 * NB - 1, 1)

            bx, bg, be, bo, by, bl, blt = bank[0], bank[1:3], bank[3], bank[4], bank[5], bank[6], bank[7]

            def triangle(eb, par, h, resident):
                if h == 0:
                    pe.wait_ge(b_lr[par], 32 * (eb // 2) + 32)
                    if resident:
                        pe.wait_ge(b_res[par], (eb // (NBLK * CB)) * 16 * CB // 2 + 16 * ((eb % CB) // 2) + 16)
                await_(pe, b_triout, 2 * eb + h)
                for q in range(TU):
                    dd = h * TU + q
                    d = (eb % CB) * TB + dd
                    o = be[:, q * P:(q + 1) * P]
                    for k in range(2):
                        nc.tensor.matmul(o, right_res[:, k, ds(d, 1), :].rearrange("k o j -> k (o j)"),
                                         lr[:, par, k, dd, :], start=(k == 0), stop=False)
                    last = nc.tensor.matmul(o, lr[:, par, 3, dd, :], lr[:, par, 2, dd, :], start=False, stop=True)
                last.then_inc(b_tri, 1)

            def transpose_x2(b, h):
                pe.wait_ge(b_xh, 2 * b + h + 1)
                await_(pe, b_xn, 2 * b + h)
                if h == 0:
                    await_(pe, b_tt, 2 * (b - 1))
                for t in range(TU):
                    last = nc.tensor.transpose(bx[:, t * P:(t + 1) * P], xh[:, h, t * D:(t + 1) * D], ident[:, :])
                last.then_inc(b_xtp, 1)

            def gate(b, h):
                pe.wait_ge(b_xn, 2 * b + h + 1)
                await_(pe, b_gated, 2 * (b - 1) + h + 1)
                nc.tensor.matmul(bg[h][:, :], w_og[:, :], xnt[:, h, :], start=True, stop=True).then_inc(b_gate, 1)

            def transpose_on(b, h):
                pe.wait_ge(b_on, 2 * b + h + 1)
                await_(pe, b_onw, 2 * b + h)
                for t in range(TU):
                    last = nc.tensor.transpose(bo[:, t * P:(t + 1) * P], on[:, h, t * D:(t + 1) * D], ident[:, :])
                last.then_inc(b_otp, 1)

            def project_out(b, h):
                pe.wait_ge(b_gated, 2 * b + h + 1)
                await_(pe, b_t, 2 * b + h)
                for t in range(TU):
                    last = nc.tensor.matmul(by[:, t * D:(t + 1) * D], gated[:, h, t * P:(t + 1) * P], w_o[:, :],
                                            start=True, stop=True)
                last.then_inc(b_y, 1)

            def transpose_t(b, par, h):
                pe.wait_ge(b_t, 2 * b + h + 1)
                if h == 0:
                    pe.wait_ge(b_xn, 2 * NB if isinstance(b, int) and b == NB - 1 else 2 * b + 4)
                else:
                    pe.wait_ge(b_tt, 2 * b + 1)
                for t in range(TU):
                    last = nc.tensor.transpose(bx[:, t * P:(t + 1) * P], tout[:, par, h * TU + t, :], ident[:, :])
                last.then_inc(b_ttp, 1)

            def logits(b, h):
                pe.wait_ge(b_tt, 2 * b + h + 1)
                await_(pe, b_lgs, 2 * b + h)
                for t in range(TU):
                    at = (h * TU + t) * E
                    last = nc.tensor.matmul(bl[:, at:at + E], tt[:, h, t * P:(t + 1) * P], g_c[:, :],
                                            start=True, stop=True)
                last.then_inc(b_logit, 1)

            def transpose_logits(b):
                pe.wait_ge(b_lgs, 2 * b + 2)
                await_(pe, b_exp, b)
                for h in range(2):
                    for q in range(2):
                        at = (2 * h + q) * P
                        last = nc.tensor.transpose(blt[:, at:at + P], lgs[:, h, 2 * q * E:(2 * q + 2) * E],
                                                   ident[:, :])
                last.then_inc(b_ltp, 1)

            def step(b, par, tri=False, resident=False):
                if live(b):
                    transpose_x2(b, 0)
                if tri:
                    triangle(b + CB, par, 0, resident)
                if live(b):
                    transpose_x2(b, 1)
                    gate(b, 0)
                if live(b - 1):
                    transpose_t(b - 1, 1 - par, 0)
                if live(b):
                    transpose_on(b, 0)
                    gate(b, 1)
                if live(b - 1):
                    transpose_t(b - 1, 1 - par, 1)
                if live(b):
                    transpose_on(b, 1)
                if live(b - 1):
                    logits(b - 1, 0)
                if tri:
                    triangle(b + CB, par, 1, resident)
                if live(b - 1):
                    logits(b - 1, 1)
                if live(b):
                    project_out(b, 0)
                if live(b - 1):
                    transpose_logits(b - 1)
                if live(b):
                    project_out(b, 1)

            pe.wait_ge(a_side, 8 * NB)
            for eb in range(2):
                for h in range(2):
                    triangle(eb, eb, h, True)
            with pe.Fori(1, (CB) // 2) as eb_2:
                eb = 2 * eb_2
                for par in range(2):
                    for h in range(2):
                        triangle(eb + par, par, h, True)
            step(0, 0, True)
            step(1, 1, True)
            for lo, hi, tri, resident in [(2, 32, True, False), (32, 48, True, True), (48, 80, True, False),
                                          (80, 96, True, True), (96, 128, True, False),
                                          (128, NB - 2, False, False)]:
                with pe.Fori(lo // 2, (hi) // 2) as b_2:
                    b = 2 * b_2
                    step(b, 0, tri, resident)
                    step(b + 1, 1, tri, resident)
            for b in range(NB - 2, NB + 1):
                step(b, b % 2)

            pe.wait_ge(c_bias, 32)
            for c in range(HC):
                nc.tensor.transpose(bank[0][:, c * E:(c + 1) * E], ring32[0:E, c * P:(c + 1) * P], ident[0:E, 0:E])
            nc.tensor.transpose(bank[1][:, 0:E], ring32[0:E, HF:HF + D], ident[0:E, 0:E]).then_inc(c_btp, 1)
            pe.wait_ge(c_v, V_DIAG)
            pe.wait_ge(c_iota, 2)
            nc.tensor.matmul(bank[2][:, :], ones[0:E, 0:P], diag[0:E, :], start=True, stop=True).then_inc(c_row, 1)
            for s in range(4):
                pe.wait_ge(c_v, V_U + s)
                last = nc.tensor.matmul(bank[3][:, 0:E], u_rows[:, s, :], dtop[:, s, :], start=(s == 0), stop=(s == 3))
            last.then_inc(c_pooled, 1)
            pe.wait_ge(c_v, V_PT)

            def layer1(n, par):
                pe.wait_ge(c_w1[par], 16 * (n // 2) + 16)
                await_(pe, c_hb, n)
                for e in range(XG):
                    for c in range(HC):
                        last = nc.tensor.matmul(bank[4][:, c * XG + e:c * XG + e + 1],
                                                w1buf[:, par, e, c * P:(c + 1) * P],
                                                pooled_t[:, ds(n * XG + e, 1)], start=True, stop=True)
                last.then_inc(c_h, 1)

            def layer2(n, par):
                pe.wait_ge(c_w2[par], 16 * XG * (n // 2 + 1))
                pe.wait_ge(c_gelu, n + 1)
                for e in range(XG):
                    for c in range(HC):
                        last = nc.tensor.matmul(bank[5][:, ds(n * XG + e, 1)], w2buf[:, par, e, c * P:(c + 1) * P],
                                                hid[:, par, c * XG + e:c * XG + e + 1], start=(c == 0), stop=(c == HC - 1))
                last.then_inc(c_o, 1)

            layer1(0, 0)
            with pe.Fori(0, (NXG - 2) // 2) as n_2:
                n = 2 * n_2
                layer1(n + 1, 1)
                layer2(n, 0)
                layer1(n + 2, 0)
                layer2(n + 1, 1)
            layer1(NXG - 1, 1)
            layer2(NXG - 2, 0)
            layer2(NXG - 1, 1)
            pe.wait_ge(c_v, V_OT)
            nc.tensor.transpose(bank[6][0:E, 0:D], out_t[:, :], ident[:, :]).then_inc(c_otp, 1)
            pe.wait_ge(c_v, V_OE)
            for s in range(4):
                last = nc.tensor.matmul(bank[7][:, s * D:(s + 1) * D], share[0:E, s * P:(s + 1) * P], out_e[0:E, :],
                                        start=True, stop=True)
            last.then_inc(c_delta, 1)

        @block.scalar
        def _(act):
            nw, nb_, ow, ob = (cols[:, n:n + 1] for n in range(4))

            def out_of_x(u, h):
                act.wait_ge(a_tp, u + 1)
                await_(act, a_lr, 4 * (u - 1))
                nc.scalar.activation(xnt[:, h, :], bank[h][:, :], ACT.Identity, bias=nb_, scale=nw
                                     ).then_inc(a_xn, 1)

            def sigmoids(u, h):
                for j in range(2):
                    for t in range(2):
                        act.wait_ge(a_lr, 4 * u + 2 * j + t + 1)
                        await_(act, a_side, 4 * (u - 1) + 2 * j + t + 1)
                        nc.scalar.activation(sig[:, j, t, :], bank[2 + 2 * j + t][:, 2 * D:4 * D], ACT.Sigmoid
                                             ).then_inc(a_sig, 1)

            act.wait_ge(s_wload, 16 * 14)
            act.wait_ge(s_wcopy, 17)
            out_of_x(0, 0)
            for b in range(2):
                out_of_x(2 * b + 1, 1)
                sigmoids(2 * b, 0)
                out_of_x(2 * b + 2, 0)
                sigmoids(2 * b + 1, 1)
            with act.Fori(2, NB - 1, 1) as b:
                out_of_x(2 * b + 1, 1)
                sigmoids(2 * b, 0)
                out_of_x(2 * b + 2, 0)
                sigmoids(2 * b + 1, 1)
            out_of_x(2 * NB - 1, 1)
            sigmoids(2 * NB - 2, 0)
            sigmoids(2 * NB - 1, 1)

            bx, bg, be, bo, blt = bank[0], bank[1:3], bank[3], bank[4], bank[7]

            def out_of_triangle(b, h):
                eb = b + CB
                c = eb // CB
                act.wait_ge(b_tri, 2 * eb + h + 1)
                await_(act, b_on, 2 * CB * (b // CB))
                nc.scalar.activation(
                    tri[:, ds(c % 2, 1), :, ds((eb % CB) * TB + h * TU, TU)].rearrange("j o i d -> j (o i) d"),
                    be[:, :].rearrange("j (d i) -> j i d", d=TU), ACT.Copy).then_inc(b_triout, 1)

            def out_of_x2(b, h):
                act.wait_ge(b_xtp, 2 * b + h + 1)
                await_(act, b_gate, 2 * (b - 1) + h + 1)
                nc.scalar.activation(xnt[:, h, :], bx[:, :], ACT.Identity, bias=nb_, scale=nw).then_inc(b_xn, 1)

            def gate_tanh(b, h):
                act.wait_ge(b_gate, 2 * b + h + 1)
                nc.scalar.activation(bg[h][:, :], bg[h][:, :], ACT.Tanh, scale=0.5).then_inc(b_tanh, 1)

            def out_of_on(b, h):
                act.wait_ge(b_otp, 2 * b + h + 1)
                await_(act, b_y, 2 * (b - 1) + h + 1)
                nc.scalar.activation(gated[:, h, :], bo[:, :], ACT.Identity, bias=ob, scale=ow).then_inc(b_onw, 1)

            def out_of_t(b, h):
                act.wait_ge(b_ttp, 2 * b + h + 1)
                await_(act, b_logit, 2 * (b - 1) + h + 1)
                nc.scalar.activation(tt[:, h, :], bx[:, :], ACT.Copy).then_inc(b_tt, 1)

            def exps(b):
                act.wait_ge(b_i8, b + 1)
                await_(act, b_expsum, b)
                nc.scalar.activation(ejunk[:, :], blt[:, :], ACT.Exp, bias=negm[:, :], accum_out=esum[:, :]
                                     ).then_inc(b_exp, 1)
                act.wait_ge(b_exp, b + 1)
                nc.scalar.activation(csum[:, ds(b, 1)], esum[:, :], ACT.Copy).then_inc(b_expsum, 1)

            def step(b, tri=False):
                if live(b):
                    out_of_x2(b, 0)
                if tri:
                    out_of_triangle(b, 0)
                if live(b):
                    out_of_x2(b, 1)
                    gate_tanh(b, 0)
                if live(b - 2):
                    exps(b - 2)
                if live(b - 1):
                    out_of_t(b - 1, 0)
                if live(b):
                    out_of_on(b, 0)
                    gate_tanh(b, 1)
                if live(b - 1):
                    out_of_t(b - 1, 1)
                if live(b):
                    out_of_on(b, 1)
                if tri:
                    out_of_triangle(b, 1)

            act.wait_ge(a_store, 32 * NCH)
            with act.Fori(0, CB, 1) as eb0:
                for h in range(2):
                    act.wait_ge(b_tri, 2 * eb0 + h + 1)
                    nc.scalar.activation(tri[:, 0, :, ds(eb0 * TB + h * TU, TU)],
                                         be[:, :].rearrange("j (d i) -> j i d", d=TU), ACT.Copy
                                         ).then_inc(b_triout, 1)
            step(0, True)
            step(1, True)
            with act.Fori(2, NB - CB, 1) as b:
                step(b, True)
            with act.Fori(NB - CB, NB, 1) as b:
                step(b)
            for b in range(NB, NB + 2):
                step(b)

            act.wait_ge(c_v, V_TOP)
            nc.scalar.activation(wexp[:, :], cand[:, :, 0], ACT.Exp, bias=negtop[:, :]).then_inc(c_act, 1)
            act.wait_ge(c_v, V_M2)
            nc.scalar.activation(hm[0:E, :], both[0:E, :, 16], ACT.Exp, bias=neg2[0:E, :]).then_inc(c_act, 1)
            nc.scalar.activation(ev[0:E, :], v8[0:E, :], ACT.Exp, bias=neg2[0:E, :]).then_inc(c_act, 1)

            def gelus(n, par):
                act.wait_ge(c_hb, n + 1)
                await_(act, c_o, n - 1)
                nc.scalar.activation(hid[:, par, :], hpre[:, par, :], ACT.Gelu).then_inc(c_gelu, 1)

            gelus(0, 0)
            gelus(1, 1)
            with act.Fori(1, (NXG) // 2) as n_2:
                n = 2 * n_2
                gelus(n, 0)
                gelus(n + 1, 1)

        @block.vector
        def _(dve):
            dests = [w_lr[:, n * D:(n + 1) * D] for n in range(4)] + [w_og[:, :]]
            for n in range(15):
                dve.wait_ge(s_wt, n + 1)
                src = bank[n % 2][:, 0:P]
                if n < 5:
                    nc.vector.tensor_copy(dests[n], src).then_inc(s_wcopy, 1)
                elif n == 5:
                    nc.vector.tensor_scalar(w_o[:, :], src, 0.5, None, ALU.mult).then_inc(s_wcopy, 1)
                else:
                    m = n - 6
                    nc.vector.tensor_copy(mask_t[:, m % NBLK, (m // NBLK) * P:(m // NBLK + 1) * P], src
                                          ).then_inc(s_wcopy, 1)
                if n == 5:
                    nc.vector.reduce_sum(negm[0:E, :], wraw[0:E, 6, :], axis=AX.X).then_inc(s_gmean, 1)
                    dve.wait_ge(s_gmean, 1)
                    nc.vector.tensor_scalar(tmp[0:E, 0, 0:1], negm[0:E, :], 1.0 / D, None, ALU.mult
                                            ).then_inc(s_gmean, 1)
                    dve.wait_ge(s_gmean, 2)
                    nc.vector.tensor_scalar(wraw[0:E, 7, :], wraw[0:E, 6, :], tmp[0:E, 0, 0:1], None,
                                            ALU.subtract).then_inc(s_gcen, 1)
            dve.wait_ge(s_wt, 16)
            nc.vector.tensor_copy(g_c[:, :], bank[1][:, 0:E]).then_inc(s_wcopy, 2)

            def moments(src, b, dst, s_bn, s_1, s_2, s_out):
                for t in range(TB):
                    last = nc.vector.bn_stats(bst[:, t, :], src(t))
                last.then_inc(s_bn, 1)
                dve.wait_ge(s_bn, b + 1)
                nc.vector.tensor_tensor(tmp[:, 0, :], bst[:, :, 1], bst[:, :, 4], ALU.subtract).then_inc(s_1, 1)
                nc.vector.tensor_tensor(dst[:, 0, :], bst[:, :, 1], bst[:, :, 4], ALU.add)
                nc.vector.tensor_tensor(tmp[:, 1, :], bst[:, :, 2], bst[:, :, 5], ALU.add)
                dve.wait_ge(s_1, b + 1)
                nc.vector.scalar_tensor_tensor(tmp[:, 2, :], tmp[:, 0, :], D / 4.0, tmp[:, 0, :], ALU.mult, ALU.mult
                                               ).then_inc(s_2, 1)
                dve.wait_ge(s_2, b + 1)
                nc.vector.tensor_tensor(dst[:, 1, :], tmp[:, 1, :], tmp[:, 2, :], ALU.add).then_inc(s_out, 1)

            def stats_x(b, par):
                dve.wait_ge(a_x[par], 16 * (b // 2) + 16)
                moments(lambda t: xin[:, par, t, :], b, sm[:, par, :, :], a_bn, a_s1, a_s2, a_sm)

            def stage_sides(b, stored):
                if stored:
                    dve.wait_ge(a_store, 32 * ((b - CB // 2) // CB))
                c = b // CB
                for n in range(TB):
                    dve.wait_ge(a_sig, TB * b + n + 1)
                    i = (b % RB) * TB + n
                    il = (b % CB) * TB + n
                    nc.vector.scalar_tensor_tensor(
                        stage[:, ds(c % 2, 1), :, :, ds(il, 1)].rearrange("k o s d i -> k (o s) (d i)"),
                        bank[2 + n % 4][:, 0:2 * D].rearrange("k (s d) -> k s d", s=2),
                        mask_t[:, ds(b // RB, 1), ds(i, 1)].rearrange("k o i -> k (o i)"),
                        sig[:, (n // 2) % 2, n % 2, :].rearrange("k (s d) -> k s d", s=2),
                        ALU.mult, ALU.mult).then_inc(a_side, 1)

            dve.wait_ge(s_wcopy, 17)
            stats_x(0, 0)
            for b in range(2):
                stats_x(b + 1, (b + 1) % 2)
                stage_sides(b, False)
            for lo, hi, stored in [(2, 24, False), (24, NB - 2, True)]:
                with dve.Fori(lo // 2, (hi) // 2) as b_2:
                    b = 2 * b_2
                    for par in range(2):
                        stats_x(b + par + 1, 1 - par)
                        stage_sides(b + par, stored)
            stats_x(NB - 1, 1)
            stage_sides(NB - 2, True)
            stage_sides(NB - 1, True)

            bg, by, bl, blt = bank[1:3], bank[5], bank[6], bank[7]

            def maxima(b):
                dve.wait_ge(b_ltp, b + 1)
                pass_on(dve, s_dve)
                nc.vector.max(m8[:, :], blt[:, :]).then_inc(b_m8, 1)
                dve.wait_ge(b_m8, b + 1)
                await_(dve, b_exp, b)
                nc.vector.tensor_scalar(negm[:, :], m8[:, 0:1], -1.0, None, ALU.mult).then_inc(b_negm, 1)
                nc.vector.tensor_copy(cand[:, ds(b, 1), :], m8[:, :].rearrange("p (o k) -> p o k", o=1))
                nc.vector.max_index(i8[:, :], m8[:, :], blt[:, :]).then_inc(b_i8, 1)
                dve.wait_ge(b_i8, b + 1)
                nc.vector.tensor_copy(cidx[:, ds(b, 1), :], i8[:, :].rearrange("p (o k) -> p o k", o=1)
                                      ).then_inc(b_keep, 1)

            def stats_t(b, par):
                dve.wait_ge(b_t, 2 * b + 2)
                moments(lambda t: tout[:, par, t, :], b, smt, b_bnt, b_t1, b_t2, b_smt)

            def gates(b, h):
                dve.wait_ge(b_tanh, 2 * b + h + 1)
                dve.wait_ge(b_onw, 2 * b + h + 1)
                nc.vector.scalar_tensor_tensor(gated[:, h, :], bg[h][:, :], 1.0, gated[:, h, :], ALU.add, ALU.mult
                                               ).then_inc(b_gated, 1)

            def scale_logits(b, h):
                dve.wait_ge(b_logit, 2 * b + h + 1)
                dve.wait_ge(b_rst, b + 1)
                await_(dve, b_ltp, b)
                nc.vector.tensor_tensor(
                    lgs[:, h, :].rearrange("p (t e) -> p t e", t=TU),
                    bl[:, h * TU * E:(h + 1) * TU * E].rearrange("p (t e) -> p t e", t=TU),
                    tst[:, 1, h * TU:(h + 1) * TU].unsqueeze(2).broadcast_to([P, TU, E]), ALU.mult
                ).then_inc(b_lgs, 1)

            def residual(b, par, h):
                dve.wait_ge(b_y, 2 * b + h + 1)
                if h == 0:
                    await_(dve, b_store[par], 16 * (b // 2))
                await_(dve, b_ttp, 2 * (b - 2) + h + 1)
                nc.vector.tensor_tensor(tout[:, par, h * TU:(h + 1) * TU, :],
                                        by[:, :].rearrange("p (t d) -> p t d", t=TU),
                                        xin[:, par, h * TU:(h + 1) * TU, :], ALU.add).then_inc(b_t, 1)

            def tri_tile(b, t):
                return tri[:, ds((b // CB) % 2, 1), ds((b % CB) * TB + t, 1), :].rearrange("j o i d -> j (o i d)")

            def stats_o(b):
                dve.wait_ge(b_triout, 2 * CB * (b // CB) + 2 * CB)
                moments(lambda t: tri_tile(b, t), b, smo, b_bno, b_o1, b_o2, b_smo)

            def norm_o(b):
                dve.wait_ge(b_ost, b + 1)
                for h in range(2):
                    await_(dve, b_otp, 2 * (b - 1) + h + 1)
                    for t in range(TU):
                        n = h * TU + t
                        last = nc.vector.tensor_scalar(on[:, h, t * D:(t + 1) * D], tri_tile(b, n),
                                                       ost[:, 0, n:n + 1], ost[:, 1, n:n + 1], ALU.add, ALU.mult)
                    last.then_inc(b_on, 1)

            def step(b, par):
                if live(b - 2):
                    maxima(b - 2)
                if live(b - 1):
                    stats_t(b - 1, 1 - par)
                if live(b):
                    gates(b, 0)
                    gates(b, 1)
                if live(b - 1):
                    scale_logits(b - 1, 0)
                if live(b + 1):
                    stats_o(b + 1)
                if live(b - 1):
                    scale_logits(b - 1, 1)
                if live(b):
                    residual(b, par, 0)
                    residual(b, par, 1)
                if live(b + 1):
                    norm_o(b + 1)

            stats_o(0)
            norm_o(0)
            step(0, 0)
            step(1, 1)
            with dve.Fori(1, (NB - 2) // 2) as b_2:
                b = 2 * b_2
                step(b, 0)
                step(b + 1, 1)
            for b in range(NB - 2, NB + 2):
                step(b, b % 2)

            count = [0]

            def done(ins):
                count[0] += 1
                ins.then_inc(c_v, 1)
                dve.wait_ge(c_v, count[0])

            def mark(value):
                assert count[0] == value, (count[0], value)

            dve.wait_ge(b_expsum, NB)
            dve.wait_ge(b_keep, NB)
            cflat = cand[:, :, :].rearrange("p b k -> p (b k)")
            iflat = cidx[:, :, :].rearrange("p b k -> p (b k)")
            done(nc.vector.memset(par384[0:E, :], 0.0))
            done(nc.vector.memset(par384[E:2 * E, :], float(N)))
            done(nc.vector.tensor_scalar(cflat, cflat, gb[:, :], None, ALU.add))
            done(nc.vector.max(both[:, 0, 0:8], cflat))
            done(nc.vector.tensor_scalar(negtop[:, :], both[:, 0, 0:1], -1.0, None, ALU.mult))
            mark(V_TOP)
            done(nc.vector.max_index(pos_i[:, :], both[:, 0, 0:8], cflat))
            done(nc.vector.tensor_copy(pos_f[:, :], pos_i[:, :]))
            dve.wait_ge(c_iota, 1)
            done(nc.vector.tensor_copy(iota_f, iota_i))
            for k in range(K):
                last = nc.vector.scalar_tensor_tensor(pick, iota_f, pos_f[:, k:k + 1], iflat, ALU.is_equal, ALU.mult,
                                                      accum_out=raw[:, k:k + 1])
                if k < K - 1:
                    done(last)
            done(last)
            done(nc.vector.tensor_copy(raw_i[:, :], raw[:, :]))
            done(nc.vector.tensor_scalar(bi[:, :], pos_i[:, :], 3, None, ALU.logical_shift_right))
            done(nc.vector.tensor_scalar(qi[:, :], raw_i[:, :], 7, None, ALU.logical_shift_right))
            done(nc.vector.tensor_copy(bf[:, :], bi[:, :]))
            done(nc.vector.tensor_copy(qf[:, :], qi[:, :]))
            done(nc.vector.scalar_tensor_tensor(tok[:, :], qf[:, :], float(2 * N - P), raw[:, :], ALU.mult, ALU.add))
            done(nc.vector.scalar_tensor_tensor(tok[:, :], bf[:, :], float(TB * N), tok[:, :], ALU.mult, ALU.add))
            dve.wait_ge(c_iota, 2)
            done(nc.vector.tensor_scalar(tok[:, :], tok[:, :], par384[:, :], None, ALU.add))
            for m in range(1, NBLK):
                done(nc.vector.tensor_scalar(qf[:, :], bf[:, :], float(m * RB), float(P - S), ALU.is_ge, ALU.mult))
                done(nc.vector.tensor_tensor(both[:, 0, 8:16] if m == NBLK - 1 else tok[:, :], tok[:, :], qf[:, :],
                                             ALU.add))
            done(nc.vector.tensor_copy(both[:, 0, 16:17], both[:, 0, 0:1]))
            dve.wait_ge(c_act, 1)
            done(nc.vector.tensor_tensor(wexp[:, :], wexp[:, :], csum[:, :], ALU.mult))
            done(nc.vector.reduce_sum(both[:, 0, 17:18], wexp[:, :], axis=AX.X))
            mark(V_FIN)
            dve.wait_ge(c_half, 16)
            done(nc.vector.tensor_copy(v16[0:E, :, :], both[0:E, :, 0:8]))
            done(nc.vector.tensor_copy(t16[0:E, :, :], both[0:E, :, 8:16]))
            v16f = v16[0:E, :, :].rearrange("p s k -> p (s k)")
            t16f = t16[0:E, :, :].rearrange("p s k -> p (s k)")
            done(nc.vector.max(v8[0:E, :], v16f))
            done(nc.vector.tensor_scalar(neg2[0:E, :], v8[0:E, 0:1], -1.0, None, ALU.mult))
            mark(V_M2)
            done(nc.vector.max_index(pos_i[0:E, :], v8[0:E, :], v16f))
            done(nc.vector.tensor_copy(pos_f[0:E, :], pos_i[0:E, :]))
            for k in range(K):
                done(nc.vector.scalar_tensor_tensor(pick[0:E, 0:16], iota_f[0:E, 0:16], pos_f[0:E, k:k + 1], t16f,
                                                    ALU.is_equal, ALU.mult, accum_out=kv[0:E, 0, k:k + 1]))
            dve.wait_ge(c_act, 3)
            done(nc.vector.tensor_tensor(hm[0:E, :], hm[0:E, :], both[0:E, :, 17], ALU.mult))
            done(nc.vector.reduce_sum(den[0:E, :], hm[0:E, :], axis=AX.X))
            done(nc.vector.reciprocal(den[0:E, :], den[0:E, :]))
            done(nc.vector.tensor_scalar(kv[0:E, 1, :], ev[0:E, :], den[0:E, :], None, ALU.mult))
            mark(V_KV)
            done(nc.vector.tensor_tensor(
                diag[0:E, :].rearrange("p (k e) -> p k e", k=K),
                ident[0:E, 0:E].unsqueeze(1).broadcast_to([E, K, E]),
                kv[0:E, 0, :].unsqueeze(2).broadcast_to([E, K, E]), ALU.mult))
            mark(V_DIAG)
            dve.wait_ge(c_kv, 16)
            for half in range(2):
                sl = slice(half * E, (half + 1) * E)
                done(nc.vector.tensor_copy(sel[sl, :, :],
                                           kv[sl, :, :].rearrange("p v (s h) -> p v s h", h=2)[:, :, :, half]))
            done(nc.vector.tensor_copy(idx_i[:, :], sel[:, 0, :]))
            mark(V_IDX)
            dve.wait_ge(c_row, 1)
            done(nc.vector.tensor_copy(idx_row[:, :], bank[2][:, :]))
            done(nc.vector.tensor_scalar(share[0:E, :], idx_row[0:E, :], kv[0:E, 0, 0:1], kv[0:E, 1, 0:1],
                                         ALU.is_equal, ALU.mult))
            for k in range(1, K):
                done(nc.vector.tensor_scalar(part[0:E, :], idx_row[0:E, :], kv[0:E, 0, k:k + 1], kv[0:E, 1, k:k + 1],
                                             ALU.is_equal, ALU.mult))
                done(nc.vector.tensor_tensor(share[0:E, :], share[0:E, :], part[0:E, :], ALU.add))
            done(nc.vector.tensor_copy(id2[0:E, :], ident[0:E, 0:E]))
            done(nc.vector.tensor_copy(id2[E:2 * E, :], ident[E:2 * E, E:2 * E]))
            for s in range(4):
                done(nc.vector.tensor_scalar(dtop[:, s, :], id2[:, :], sel[:, 1, s:s + 1], None, ALU.mult))
            dve.wait_ge(c_gather, 64)
            for s in range(4):
                done(nc.vector.bn_stats(bst[:, s, :], t_rows[:, s, :]))
            for s in range(4):
                done(nc.vector.bn_aggr(mv4[:, s, :], bst[:, s, :]))
            mark(V_VAR)
            dve.wait_ge(c_pool, 2)
            for s in range(4):
                done(nc.vector.tensor_scalar(u_rows[:, s, :], t_rows[:, s, :], mv4[:, s, 0:1], rst4[:, s:s + 1],
                                             ALU.subtract, ALU.mult))
                mark(V_U + s)
            dve.wait_ge(c_btp, 1)
            done(nc.vector.tensor_copy(b1_t, bank[0][:, 0:HC * E]))
            done(nc.vector.tensor_copy(b2_t, bank[1][:, 0:E]))
            dve.wait_ge(c_iota, 3)
            dve.wait_ge(c_pooled, 1)
            done(nc.vector.tensor_copy(pooled_t[:, :], bank[3][:, 0:E]))
            mark(V_PT)
            for s in range(4):
                done(nc.vector.scalar_tensor_tensor(part[:, :], idx_row[:, :], sel[:, 0, s:s + 1], earlier[:, s, :],
                                                    ALU.is_equal, ALU.mult, accum_out=dup[:, s:s + 1]))
            done(nc.vector.scalar_tensor_tensor(dup[:, :], dup[:, :], float(S), sel[:, 0, :], ALU.mult, ALU.add))
            done(nc.vector.tensor_copy(idx_w[:, :], dup[:, :]))

            def hidden(n, par):
                dve.wait_ge(c_h, n + 1)
                await_(dve, c_gelu, n - 1)
                nc.vector.tensor_tensor(
                    hpre[:, par, :].rearrange("p (c e) -> p c e", c=HC),
                    bank[4][:, 0:HC * XG].rearrange("p (c e) -> p c e", c=HC),
                    b1_t.rearrange("p (c e) -> p c e", c=HC)[:, :, ds(n * XG, XG)], ALU.add).then_inc(c_hb, 1)

            hidden(0, 0)
            hidden(1, 1)
            with dve.Fori(1, (NXG) // 2) as n_2:
                n = 2 * n_2
                hidden(n, 0)
                hidden(n + 1, 1)
            dve.wait_ge(c_o, NXG)
            done(nc.vector.tensor_tensor(out_t[:, :], bank[5][:, 0:E], b2_t, ALU.add))
            mark(V_OT)
            dve.wait_ge(c_otp, 1)
            done(nc.vector.tensor_copy(out_e[0:E, :], bank[6][0:E, 0:D]))
            mark(V_OE)
            dve.wait_ge(c_delta, 1)
            done(nc.vector.tensor_tensor(new_rows[:, :, :], bank[7][:, :].rearrange("p (s d) -> p s d", s=4),
                                         t_rows[:, :, :], ALU.add))
            mark(V_NEW)


_INS = ['x', 'L0_conv_mask', 'L0_conv_norm_w', 'L0_conv_norm_b', 'L0_conv_W_left', 'L0_conv_W_right',
        'L0_conv_W_left_gate', 'L0_conv_W_right_gate', 'L0_conv_W_out_gate', 'L0_conv_out_norm_w',
        'L0_conv_out_norm_b', 'L0_conv_W_out', 'L0_ffn_gate_w', 'L0_ffn_gate_b', 'L0_ffn_weight1',
        'L0_ffn_weight2']


def kernel(**inputs):
    import numpy as _np
    import concourse.bacc as _bacc
    from concourse import mybir as _mybir
    from concourse.bass_utils import run_bass_kernel_spmd as _run

    nc = _bacc.Bacc("TRN2", target_bir_lowering=False, num_devices=1)
    arrays, args = {}, []
    for name in _INS:
        a = _np.ascontiguousarray(inputs[name])
        arrays[f"in_{name}_dram"] = a
        args.append(nc.dram_tensor(f"in_{name}_dram", a.shape, _mybir.dt.from_np(a.dtype), kind="ExternalInput").ap())
    shape = inputs["x"].shape
    args.append(nc.dram_tensor("out_0_dram", shape, _mybir.dt.float32, kind="ExternalOutput").ap())
    metaformer_layer_kernel(nc, *args)
    r = _run(nc, [arrays], core_ids=[0])
    return r.results[0]["out_0_dram"]
```

```python
import concourse.bass as bass
from concourse import mybir
from contextlib import ExitStack


def metaformer_layer_kernel(
    nc: bass.Bass,
    x: bass.AP,
    mask: bass.AP,
    norm_w: bass.AP,
    norm_b: bass.AP,
    W_left: bass.AP,
    W_right: bass.AP,
    W_left_gate: bass.AP,
    W_right_gate: bass.AP,
    W_out_gate: bass.AP,
    out_norm_w: bass.AP,
    out_norm_b: bass.AP,
    W_out: bass.AP,
    gate_w: bass.AP,
    gate_b: bass.AP,
    weight1: bass.AP,
    weight2: bass.AP,
    out: bass.AP,
):
    fp32 = mybir.dt.float32
    bf16 = mybir.dt.bfloat16
    u32 = mybir.dt.uint32
    i32 = mybir.dt.int32
    ALU = mybir.AluOpType
    ACT = mybir.ActivationFunctionType
    AX = mybir.AxisListType
    ds = bass.ds

    P = 128
    N = x.shape[1]
    D = x.shape[3]
    E = gate_w.shape[0]
    HF = weight1.shape[2]
    K = 8
    S = N * N
    NBLK = N // P
    TB = 8
    TU = TB // 2
    RB = N // TB
    NB = NBLK * RB
    CB = P // TB
    NCH = NB // CB
    EPS_C = 1e-6
    EPS = 1e-5
    HC = HF // P
    XG = 8
    NXG = E // XG

    x3 = x[0]
    mask2 = mask[0]
    out3 = out[0]
    rows = out[0].rearrange("i j d -> (i j) d")

    ctx = ExitStack()
    with ctx:
        def sb(name, shape, dt):
            return ctx.enter_context(nc.sbuf_tensor(name, shape, dt))

        def pb(name, shape, dt):
            return ctx.enter_context(nc.psum_tensor(name, shape, dt))

        def sem(name):
            return ctx.enter_context(nc.semaphore(name))

        sides = nc.dram_tensor("sides", (2, NBLK, NBLK, P, D * P), bf16, kind="Internal").ap()

        arena = sb("arena", [P, 4 * D * P], bf16)
        stage = arena[:, :].rearrange("k (c s d i) -> k c s d i", c=2, s=2, d=D)
        right_res = arena[:, 0:2 * D * P].rearrange("k (t d j) -> k t d j", t=2, d=D)
        tri = arena[:, 2 * D * P:4 * D * P].rearrange("j (c i d) -> j c i d", c=2, i=P)
        experts = arena[:, :].bitcast(fp32).rearrange("p (e l h) -> p e l h", l=2, h=HF)
        ring = sb("ring", [P, 2 * 4 * TB * P], bf16)
        lr = ring[:, :].rearrange("k (s q d i) -> k s q d i", s=2, q=4, d=TB)
        ring32 = ring[:, :].bitcast(fp32)
        mask_t = ring32[:, 0:NBLK * N].rearrange("k (b i) -> k b i", b=NBLK)

        work = sb("work", [P, 2 * 2 * TB * D + 5 * TB * D + TB * E + 2 * NB * TB], fp32)
        at = [0]

        def piece(*shape):
            n = 1
            for v in shape:
                n *= v
            flat = work[:, at[0]:at[0] + n]
            at[0] += n
            names = "abc"[:len(shape)]
            return flat.rearrange(f"p ({' '.join(names)}) -> p {' '.join(names)}",
                                  **{k: v for k, v in zip(names, shape)})

        tout = piece(2, TB, D)
        xin = piece(2, TB, D)
        xh, xnt, on, gated, tt = (piece(2, TU * D) for _ in range(5))
        lgs = piece(2, TU * E)
        stats = piece(2, NB * TB)
        x_slots = [xin[:, 0, :, :], xin[:, 1, :, :]] + [
            v.rearrange("p h (t d) -> p (h t) d", d=D) for v in (on, gated)]
        sig = tout[:, 0, :, :].rearrange("p (j t) d -> p j (t d)", j=2).rearrange(
            "p j (t c) -> p j t c", t=2)
        w_lr = tt[:, 0, :]
        cand = sb("cand", [P, NB, K], fp32)
        cidx = sb("cidx", [P, NB, K], mybir.dt.uint16)
        csum = sb("csum", [P, NB], fp32)
        ident = sb("ident", [P, P], fp32)
        w_og = sb("w_og", [D, D], fp32)
        w_o = sb("w_o", [D, D], fp32)
        g_c = sb("g_c", [D, E], fp32)
        cols = sb("cols", [P, 4], fp32)
        gb = sb("gb", [P, 1], fp32)
        mhalf = sb("mhalf", [P, TB], fp32)
        bst = sb("bst", [P, TB, 6], fp32)
        tmp = sb("tmp", [P, 3, TB], fp32)
        sm = sb("sm", [P, 2, 2, TB], fp32)
        xst = sb("xst", [P, 2, 2, TB], fp32)
        smt = sb("smt", [P, 2, TB], fp32)
        tst = sb("tst", [P, 2, TB], fp32)
        smo = sb("smo", [P, 2, TB], fp32)
        ost = sb("ost", [P, 3, TB], fp32)
        m8 = sb("m8", [P, K], fp32)
        negm = sb("negm", [P, 1], fp32)
        i8 = sb("i8", [P, K], u32)
        esum = sb("esum", [P, 1], fp32)
        wraw = xin[:, 0, :, :]

        used = [0]

        def carve(shape, dt=fp32):
            n = 1
            for v in shape:
                n *= v
            at = used[0]
            used[0] += n
            flat = work[:, at:at + n]
            if dt != fp32:
                flat = flat.bitcast(dt)
            if len(shape) == 2:
                return flat.rearrange("p (a b) -> p a b", a=shape[0])
            return flat

        iota_i, iota_f, pick = carve([NB * K], i32), carve([NB * K]), carve([NB * K])
        ones = carve([4 * 4 * P])
        earlier = ring32[:, HF + D:HF + D + 16 * P].rearrange("p (s a) -> p s a", s=4)
        idx_row, share, part, diag = (carve([K * E]) for _ in range(4))
        t_rows, u_rows, new_rows = (carve([4, D]) for _ in range(3))
        dtop, id2 = carve([4, E]), carve([E])
        b1_t, b2_t, pooled_t = carve([HC * E]), carve([E]), carve([E])
        hid, hpre = carve([2, HC * XG]), carve([2, HC * XG])
        out_t, out_e = carve([E]), carve([D])
        wexp = carve([NB])
        both, kv, sel = carve([2, 18]), carve([2, K]), carve([2, 4])
        v16, t16 = carve([2, K]), carve([2, K])
        pos_i, raw_i, bi, qi = (carve([K], u32) for _ in range(4))
        pos_f, raw, bf, qf, tok, v8, ev = (carve([K]) for _ in range(7))
        idx_i, idx_w = carve([4], i32), carve([4], i32)
        mv4, rst4, dup = carve([4, 2]), carve([4]), carve([4])
        hm, den = carve([2]), carve([1])
        par384, negtop, neg2 = carve([1]), carve([1]), carve([1])
        V_TOP, V_FIN, V_M2, V_KV, V_DIAG, V_IDX = 5, 31, 35, 49, 50, 53
        V_VAR, V_U, V_PT, V_OT, V_OE, V_NEW = 83, 84, 90, 97, 98, 99

        bank = [pb(f"bank{i}", [P, 512], fp32) for i in range(8)]

        s_ident = sem("s_ident")
        s_const = sem("s_const")
        s_pool = sem("s_pool")
        s_dve = sem("s_dve")
        s_sp = sem("s_sp")
        s_wload = sem("s_wload")
        s_wt = sem("s_wt")
        s_wcopy = sem("s_wcopy")
        s_gmean = sem("s_gmean")
        s_gcen = sem("s_gcen")
        a_x = [sem(f"a_x{i}") for i in range(4)]
        a_bn = sem("a_bn")
        a_s1 = sem("a_s1")
        a_s2 = sem("a_s2")
        a_sm = sem("a_sm")
        a_arg = sem("a_arg")
        a_pow = sem("a_pow")
        a_keep = sem("a_keep")
        a_xh = sem("a_xh")
        a_tp = sem("a_tp")
        a_xn = sem("a_xn")
        a_lr = sem("a_lr")
        a_sig = sem("a_sig")
        a_side = sem("a_side")
        a_store = sem("a_store")
        b_x = [[sem(f"b_x{i}{h}") for h in range(2)] for i in range(2)]
        b_lr = [sem(f"b_lr{i}") for i in range(2)]
        b_resfirst = sem("b_resfirst")
        b_res = [sem(f"b_res{i}") for i in range(2)]
        b_store = [sem(f"b_store{i}") for i in range(2)]
        b_xst = sem("b_xst")
        b_xh = sem("b_xh")
        b_xtp = sem("b_xtp")
        b_xn = sem("b_xn")
        b_gate = sem("b_gate")
        b_tanh = sem("b_tanh")
        b_tri = sem("b_tri")
        b_triout = sem("b_triout")
        b_bno = sem("b_bno")
        b_o1 = sem("b_o1")
        b_o2 = sem("b_o2")
        b_smo = sem("b_smo")
        b_oarg = sem("b_oarg")
        b_ost = sem("b_ost")
        b_ost1 = sem("b_ost1")
        b_on = sem("b_on")
        b_on1 = sem("b_on1")
        b_otp = sem("b_otp")
        b_onw = sem("b_onw")
        b_gated = sem("b_gated")
        b_y = sem("b_y")
        b_t = sem("b_t")
        b_bnt = sem("b_bnt")
        b_t1 = sem("b_t1")
        b_t2 = sem("b_t2")
        b_smt = sem("b_smt")
        b_targ = sem("b_targ")
        b_rst = sem("b_rst")
        b_ttp = sem("b_ttp")
        b_tt = sem("b_tt")
        b_logit = sem("b_logit")
        b_lgs = sem("b_lgs")
        b_ltp = sem("b_ltp")
        b_m8 = sem("b_m8")
        b_negm = sem("b_negm")
        b_i8 = sem("b_i8")
        b_keep = sem("b_keep")
        b_exp = sem("b_exp")
        c_early = sem("c_early")
        c_w = [sem(f"c_w{i}") for i in range(4)]
        c_bias = sem("c_bias")
        c_iota = sem("c_iota")
        c_v = sem("c_v")
        c_act = sem("c_act")
        c_half = sem("c_half")
        c_kv = sem("c_kv")
        c_pool = sem("c_pool")
        c_row = sem("c_row")
        c_gather = sem("c_gather")
        c_btp = sem("c_btp")
        c_pooled = sem("c_pooled")
        c_h = sem("c_h")
        c_hb = sem("c_hb")
        c_gelu = sem("c_gelu")
        c_o = sem("c_o")
        c_otp = sem("c_otp")
        c_delta = sem("c_delta")
        c_scatter = sem("c_scatter")

        def live(n):
            return not isinstance(n, int) or 0 <= n < NB

        def await_(eng, s, v):
            if not isinstance(v, int) or v > 0:
                eng.wait_ge(s, v)

        def pass_on(eng, s):
            eng.sem_inc(s, 1)

        def rows_of(b):
            return ds((b % RB) * TB, TB)

        def cols_of(b):
            return ds((b // RB) * P, P)

        block = ctx.enter_context(nc.Block())

        @block.sync
        def _(sp):
            for n, w in enumerate([W_left, W_right, W_left_gate, W_right_gate, W_out_gate, W_out]):
                sp.dma_start(wraw[:, n, :], w).then_inc(s_wload, 16)
            sp.dma_start(wraw[0:E, 6, :], gate_w).then_inc(s_wload, 16)
            for n, w in enumerate([norm_w, norm_b, out_norm_w, out_norm_b]):
                sp.dma_start(cols[:, n:n + 1], w.rearrange("(d o) -> d o", o=1)).then_inc(s_wload, 16)
            for h in range(2):
                sp.dma_start(gb[h * E:(h + 1) * E, :], gate_b.rearrange("(d o) -> d o", o=1)).then_inc(s_wload, 16)
            sp.dma_start(tout[:, :, :, :].rearrange("p s t d -> p (s t d)")[:, 0:NBLK * N].rearrange(
                "p (b k) -> p b k", b=NBLK), mask2.rearrange("(b i) k -> i b k", b=NBLK)).then_inc(s_wload, 16)

            def load_x(b, slot):
                await_(sp, a_xh, 2 * (b - 4) + 2)
                sp.dma_start(x_slots[slot], x3[rows_of(b), cols_of(b), :].rearrange("i j d -> j i d")
                             ).then_inc(a_x[slot], 16)

            def load_xs(lo, hi):
                with sp.Fori(lo // 4, hi // 4) as q:
                    for slot in range(4):
                        load_x(4 * q + slot, slot)

            sp.wait_ge(s_wcopy, 17)
            for b in range(4):
                load_x(b, b)
            for c in range(NCH):
                if c < NCH - 1:
                    load_xs(CB * c + 4, CB * (c + 1) + 4)
                else:
                    load_xs(CB * c + 4, CB * c + 8)
                    sp.wait_ge(a_store, 32 * c)
                    for g in range(4):
                        sp.dma_start(
                            right_res[:, :, g * D // 4:(g + 1) * D // 4, :].rearrange("k t d j -> k t (d j)"),
                            sides[1, 0:2, 0, :, g * D * P // 4:(g + 1) * D * P // 4].rearrange("t k n -> k t n")
                        ).then_inc(b_resfirst, 16)
                        if g % 2 == 1:
                            load_xs(CB * c + 8 + 4 * (g // 2), CB * c + 12 + 4 * (g // 2))
                sp.wait_ge(a_side, P * (c + 1))
                for side in range(2):
                    sp.dma_start(sides[side, c // NBLK, c % NBLK],
                                 stage[:, (c + 1) % 2, side, :, :].rearrange("k d i -> k (d i)")
                                 ).then_inc(a_store, 16)
            sp.wait_ge(a_store, 32 * NCH)

            def load_lr(eb, par, resident):
                c = eb // CB
                jb, ib = c // NBLK, c % NBLK
                at = (eb % CB) * TB * P
                await_(sp, b_tri, 2 * (eb - 2) + 2)
                sp.dma_start(lr[:, par, 0:3, :, :].rearrange("k q d i -> k q (d i)"),
                             sides[0, :, ds(ib, 1), :, ds(at, TB * P)].rearrange("t o k n -> k (t o) n")
                             ).then_inc(b_lr[par], 16)
                sp.dma_start(lr[:, par, 3, :, :].rearrange("k d i -> k (d i)"),
                             sides[1, 2, ds(jb, 1), :, ds(at, TB * P)].rearrange("o k n -> k (o n)")
                             ).then_inc(b_lr[par], 16)
                if resident:
                    sp.dma_start(right_res[:, :, ds((eb % CB) * TB, TB), :].rearrange("k t d j -> k t (d j)"),
                                 sides[1, 0:2, ds(jb, 1), :, ds(at, TB * P)].rearrange("t o k n -> k (t o) n")
                                 ).then_inc(b_res[par], 16)

            def load_x2(b, par):
                await_(sp, b_xh, 2 * (b - 2) + 2)
                pass_on(sp, s_sp)
                for h in range(2):
                    await_(sp, b_t, 2 * (b - 2) + h + 1)
                    pass_on(sp, s_sp)
                    sp.dma_start(xin[:, par, h * TU:(h + 1) * TU, :],
                                 x3[ds((b % RB) * TB + h * TU, TU), cols_of(b), :].rearrange("i j d -> j i d")
                                 ).then_inc(b_x[par][h], 16)

            def store_t(b, par):
                sp.wait_ge(b_t, 2 * b + 2)
                sp.dma_start(out3[rows_of(b), cols_of(b), :].rearrange("i j d -> j i d"), tout[:, par, :, :]
                             ).then_inc(b_store[par], 16)

            load_lr(0, 0, False)
            load_lr(1, 1, False)
            load_x2(0, 0)
            load_x2(1, 1)
            with sp.Fori(1, CB // 2 + 1) as eb_2:
                for par in range(2):
                    load_lr(2 * eb_2 + par, par, False)
            LA = CB + 2
            for lo, hi, resident in [(0, 30, False), (30, 46, True), (46, 78, False), (78, 94, True),
                                     (94, NB - LA, False)]:
                with sp.Fori(lo // 2, hi // 2) as b_2:
                    b = 2 * b_2
                    for par in range(2):
                        load_lr(b + par + LA, par, resident)
                        load_x2(b + par + 2, par)
                        store_t(b + par, par)
            for b in range(NB - LA, NB - CB):
                load_x2(b + 2, b % 2)
                store_t(b, b % 2)

            def load_expert(e, slot, s_load):
                sp.dma_start(experts[:, ds(slot, 1), 0, :].rearrange("d e h -> d (e h)"),
                             weight1[ds(e, 1), 0:D, :].rearrange("e d h -> d (e h)")).then_inc(s_load, 16)
                sp.dma_start(experts[:, ds(slot, 1), 1, :].rearrange("p e (c o) -> p (e c) o", c=HC),
                             weight2[ds(e, 1), 0:HF, :].rearrange("e (c h) o -> h (e c) o", c=HC)
                             ).then_inc(s_load, 16)

            sp.wait_ge(b_tri, 2 * NB)
            sp.wait_ge(b_on, NB - CB)
            sp.wait_ge(b_on1, NB - CB)

            def early_experts(q):
                for k in range(3):
                    load_expert(3 * q + k, 3 * q + k, c_early)

            with sp.Fori(0, CB // 2 - 1) as q:
                early_experts(q)
                for par in range(2):
                    b = 2 * q + NB - CB + par
                    load_x2(b + 2, par)
                    store_t(b, par)
            early_experts(CB // 2 - 1)
            store_t(NB - 2, 0)
            store_t(NB - 1, 1)
            sp.wait_ge(b_on, NB)
            sp.wait_ge(b_on1, NB)
            with sp.Fori(0, XG) as e:
                load_expert(3 * XG + e, 3 * XG + e, c_w[3])
            sp.dma_start(ring32[0:E, 0:HF], weight1[:, D, :]).then_inc(c_bias, 16)
            sp.dma_start(ring32[0:E, HF:HF + D], weight2[:, HF, :]).then_inc(c_bias, 16)
            sp.wait_ge(c_v, V_FIN)
            sp.dma_start(both[0:E, 1, :], both[E:2 * E, 0, :]).then_inc(c_half, 16)
            sp.wait_ge(c_v, V_KV)
            sp.dma_start(kv[E:2 * E, :, :], kv[0:E, :, :]).then_inc(c_kv, 16)
            for n in range(4, NXG):
                sp.wait_ge(c_o, n - 3)
                with sp.Fori(0, XG) as e:
                    load_expert(n * XG + e, (n % 4) * XG + e, c_w[n % 4])
            sp.wait_ge(c_scatter, 64)

        @block.gpsimd
        def _(pool):
            nc.gpsimd.memset(ident[:, :], 0.0).then_inc(s_ident, 1)
            nc.gpsimd.memset(mhalf[:, :], -0.5).then_inc(s_const, 1)
            pool.wait_ge(s_ident, 1)
            nc.gpsimd.affine_select(out=ident[:, :], in_=ident[:, :], compare_op=ALU.not_equal, fill=1.0,
                                    base=0, pattern=[[-1, P]], channel_multiplier=1).then_inc(s_ident, 1)

            def norm_x(b, par, slot):
                pool.wait_ge(a_sm, b + 1)
                await_(pool, a_keep, b - 1)
                pass_on(pool, s_pool)
                nc.gpsimd.tensor_scalar(xst[:, par, 1, :], sm[:, par, 1, :], (1.0 + EPS) / D, EPS * EPS_C,
                                        ALU.mult, ALU.add).then_inc(a_arg, 1)
                nc.gpsimd.tensor_scalar(xst[:, par, 0, :], sm[:, par, 0, :], -0.5, 0.0,
                                        ALU.mult, ALU.add)
                pool.wait_ge(a_arg, b + 1)
                nc.gpsimd.tensor_tensor(xst[:, par, 1, :], xst[:, par, 1, :], mhalf[:, :], ALU.pow
                                        ).then_inc(a_pow, 1)
                pool.wait_ge(a_pow, b + 1)
                nc.gpsimd.tensor_copy(stats[:, :, ds(b * TB, TB)], xst[:, par, :, :]).then_inc(a_keep, 1)
                for h in range(2):
                    await_(pool, a_tp, 2 * (b - 1) + h + 1)
                    pass_on(pool, s_pool)
                    for t in range(TU):
                        n = h * TU + t
                        last = nc.gpsimd.tensor_scalar(xh[:, h, t * D:(t + 1) * D], x_slots[slot][:, n, :],
                                                       xst[:, par, 0, n:n + 1], xst[:, par, 1, n:n + 1],
                                                       ALU.add, ALU.mult)
                    last.then_inc(a_xh, 1)

            pool.wait_ge(s_const, 1)
            for b in range(4):
                norm_x(b, b % 2, b)
            with pool.Fori(1, NB // 4) as q:
                for slot in range(4):
                    norm_x(4 * q + slot, slot % 2, slot)

            pool.wait_ge(a_keep, NB)

            def norm_x2(b, par, h):
                if h == 0:
                    nc.gpsimd.tensor_copy(xst[:, par, :, :], stats[:, :, ds(b * TB, TB)]).then_inc(b_xst, 1)
                    pool.wait_ge(b_xst, b + 1)
                pool.wait_ge(b_x[par][h], 16 * (b // 2) + 16)
                if isinstance(b, int) and b == 0:
                    pool.wait_ge(a_tp, 2 * NB - 1 + h)
                else:
                    pool.wait_ge(b_xtp, 2 * (b - 1) + h + 1)
                pass_on(pool, s_pool)
                for t in range(TU):
                    n = h * TU + t
                    last = nc.gpsimd.tensor_scalar(xh[:, h, t * D:(t + 1) * D], xin[:, par, n, :],
                                                   xst[:, par, 0, n:n + 1], xst[:, par, 1, n:n + 1],
                                                   ALU.add, ALU.mult)
                last.then_inc(b_xh, 1)

            def stats_t(b):
                pool.wait_ge(b_smt, b + 1)
                await_(pool, b_lgs, 2 * b)
                pass_on(pool, s_pool)
                nc.gpsimd.tensor_scalar(tst[:, 1, :], smt[:, 1, :], 1.0 / D, EPS, ALU.mult, ALU.add
                                        ).then_inc(b_targ, 1)
                pool.wait_ge(b_targ, b + 1)
                nc.gpsimd.tensor_tensor(tst[:, 1, :], tst[:, 1, :], mhalf[:, :], ALU.pow).then_inc(b_rst, 1)

            def stats_o(b):
                pool.wait_ge(b_smo, b + 1)
                await_(pool, b_on, b)
                await_(pool, b_on1, b)
                pass_on(pool, s_pool)
                nc.gpsimd.tensor_scalar(ost[:, 1, :], smo[:, 1, :], 1.0 / D, EPS, ALU.mult, ALU.add
                                        ).then_inc(b_oarg, 1)
                nc.gpsimd.tensor_scalar(ost[:, 0, :], smo[:, 0, :], -0.5, 0.0, ALU.mult, ALU.add)
                pool.wait_ge(b_oarg, b + 1)
                nc.gpsimd.tensor_tensor(ost[:, 1, :], ost[:, 1, :], mhalf[:, :], ALU.pow).then_inc(b_ost, 1)
                pool.wait_ge(b_ost, b + 1)
                nc.gpsimd.tensor_tensor(ost[:, 2, :], ost[:, 0, :], ost[:, 1, :], ALU.mult).then_inc(b_ost1, 1)

            def step(b, par):
                if live(b - 1):
                    stats_t(b - 1)
                if live(b + 1):
                    norm_x2(b + 1, 1 - par, 0)
                    stats_o(b + 1)
                    norm_x2(b + 1, 1 - par, 1)

            norm_x2(0, 0, 0)
            norm_x2(0, 0, 1)
            stats_o(0)
            for b in range(4):
                step(b, b % 2)
            with pool.Fori(2, NB // 2 - 1) as b_2:
                step(2 * b_2, 0)
                step(2 * b_2 + 1, 1)
            for b in range(NB - 2, NB + 1):
                step(b, b % 2)

            pool.wait_ge(b_exp, NB)
            for par in range(2):
                pool.wait_ge(b_store[par], 16 * NB // 2)
            nc.gpsimd.iota(iota_i, [[1, NB * K]], base=0, channel_multiplier=0).then_inc(c_iota, 1)
            nc.gpsimd.memset(ones[:, :], 1.0).then_inc(c_iota, 1)
            pool.wait_ge(c_iota, 2)
            nc.gpsimd.affine_select(out=earlier, in_=ones[:, :].rearrange("p (s a) -> p s a", s=4),
                                    compare_op=ALU.is_gt, fill=0.0, base=0,
                                    pattern=[[P, 4], [-1, 4 * P]], channel_multiplier=1).then_inc(c_iota, 1)
            pool.wait_ge(c_v, V_IDX)
            for s in range(4):
                pool.indirect_dma_start(
                    out=t_rows[:, s, :], out_offset=None, in_=rows,
                    in_offset=bass.IndirectOffsetOnAxis(ap=idx_i[:, s:s + 1], axis=0)).then_inc(c_gather, 16)
            pool.wait_ge(c_v, V_VAR)
            nc.gpsimd.tensor_scalar(rst4[:, :], mv4[:, :, 1], 1.0, EPS, ALU.mult, ALU.add).then_inc(c_pool, 1)
            pool.wait_ge(c_pool, 1)
            nc.gpsimd.tensor_tensor(rst4[:, :], rst4[:, :], mhalf[:, 0:4], ALU.pow).then_inc(c_pool, 1)
            pool.wait_ge(c_v, V_NEW)
            for s in range(4):
                pool.indirect_dma_start(
                    out=rows, out_offset=bass.IndirectOffsetOnAxis(ap=idx_w[:, s:s + 1], axis=0),
                    in_=new_rows[:, s, :], in_offset=None, bounds_check=S - 1, oob_is_err=False
                ).then_inc(c_scatter, 16)
            pool.wait_ge(c_scatter, 64)

        @block.tensor
        def _(pe):
            pe.wait_ge(s_ident, 2)
            pe.wait_ge(s_wload, 16 * 14)
            for n in range(6):
                if n >= 2:
                    pe.wait_ge(s_wcopy, n - 1)
                nc.tensor.transpose(bank[n % 2][:, 0:P], wraw[:, n, :], ident[:, :]).then_inc(s_wt, 1)
            mrow = tout[:, :, :, :].rearrange("p s t d -> p (s t d)")[:, 0:NBLK * N].rearrange(
                "p (b k) -> p b k", b=NBLK)
            for n in range(NBLK * NBLK):
                pe.wait_ge(s_wcopy, n + 5)
                nc.tensor.transpose(bank[n % 2][:, 0:P], mrow[:, n // NBLK, (n % NBLK) * P:(n % NBLK + 1) * P],
                                    ident[:, :]).then_inc(s_wt, 1)
            pe.wait_ge(s_wcopy, 15)
            pe.wait_ge(s_gcen, 1)
            nc.tensor.transpose(bank[1][:, 0:E], wraw[0:E, 7, :], ident[0:E, 0:E]).then_inc(s_wt, 1)

            def transpose_x(u, h):
                pe.wait_ge(a_xh, u + 1)
                await_(pe, a_xn, u - 1)
                for t in range(TU):
                    last = nc.tensor.transpose(bank[h][:, t * P:(t + 1) * P], xh[:, h, t * D:(t + 1) * D],
                                               ident[:, :])
                last.then_inc(a_tp, 1)

            def project(u, h):
                pe.wait_ge(a_xn, u + 1)
                for t in range(TU):
                    await_(pe, a_side, 4 * (u - 1) + t + 1)
                    nc.tensor.matmul(bank[2 + t][:, :], xnt[:, h, t * P:(t + 1) * P], w_lr,
                                     start=True, stop=True).then_inc(a_lr, 1)

            pe.wait_ge(s_wcopy, 17)
            transpose_x(0, 0)
            for b in range(2):
                transpose_x(2 * b + 1, 1)
                project(2 * b, 0)
                transpose_x(2 * b + 2, 0)
                project(2 * b + 1, 1)
            with pe.Fori(2, NB - 1, 1) as b:
                transpose_x(2 * b + 1, 1)
                project(2 * b, 0)
                transpose_x(2 * b + 2, 0)
                project(2 * b + 1, 1)
            transpose_x(2 * NB - 1, 1)
            project(2 * NB - 2, 0)
            project(2 * NB - 1, 1)

            bx, bg, be, bo, by, bl, blt = bank[0], bank[1:3], bank[3], bank[4], bank[5], bank[6], bank[7]

            def triangle(eb, par, h, resident):
                if h == 0:
                    pe.wait_ge(b_lr[par], 32 * (eb // 2) + 32)
                    if resident:
                        pe.wait_ge(b_res[par], (eb // (NBLK * CB) - 1) * (16 * CB // 2) + 16 * ((eb % CB) // 2) + 16)
                await_(pe, b_triout, 2 * eb + h)
                for q in range(TU):
                    dd = h * TU + q
                    d = (eb % CB) * TB + dd
                    o = be[:, q * P:(q + 1) * P]
                    for k in range(2):
                        nc.tensor.matmul(o, right_res[:, k, ds(d, 1), :].rearrange("k o j -> k (o j)"),
                                         lr[:, par, k, dd, :], start=(k == 0), stop=False)
                    last = nc.tensor.matmul(o, lr[:, par, 3, dd, :], lr[:, par, 2, dd, :], start=False, stop=True)
                last.then_inc(b_tri, 1)

            def transpose_x2(b, h):
                pe.wait_ge(b_xh, 2 * b + h + 1)
                await_(pe, b_xn, 2 * b + h)
                if h == 0:
                    await_(pe, b_tt, 2 * (b - 1))
                for t in range(TU):
                    last = nc.tensor.transpose(bx[:, t * P:(t + 1) * P], xh[:, h, t * D:(t + 1) * D], ident[:, :])
                last.then_inc(b_xtp, 1)

            def gate(b, h):
                pe.wait_ge(b_xn, 2 * b + h + 1)
                await_(pe, b_gated, 2 * (b - 1) + h + 1)
                nc.tensor.matmul(bg[h][:, :], w_og[:, :], xnt[:, h, :], start=True, stop=True).then_inc(b_gate, 1)

            def transpose_on(b, h):
                pe.wait_ge(b_on1 if h else b_on, b + 1)
                await_(pe, b_onw, 2 * b + h)
                for t in range(TU):
                    last = nc.tensor.transpose(bo[:, t * P:(t + 1) * P], on[:, h, t * D:(t + 1) * D], ident[:, :])
                last.then_inc(b_otp, 1)

            def project_out(b, h):
                pe.wait_ge(b_gated, 2 * b + h + 1)
                await_(pe, b_t, 2 * b + h)
                for t in range(TU):
                    last = nc.tensor.matmul(by[:, t * D:(t + 1) * D], gated[:, h, t * P:(t + 1) * P], w_o[:, :],
                                            start=True, stop=True)
                last.then_inc(b_y, 1)

            def transpose_t(b, par, h):
                pe.wait_ge(b_t, 2 * b + h + 1)
                if h == 0:
                    pe.wait_ge(b_xn, 2 * NB if isinstance(b, int) and b == NB - 1 else 2 * b + 4)
                else:
                    pe.wait_ge(b_tt, 2 * b + 1)
                for t in range(TU):
                    last = nc.tensor.transpose(bx[:, t * P:(t + 1) * P], tout[:, par, h * TU + t, :], ident[:, :])
                last.then_inc(b_ttp, 1)

            def logits(b, h):
                pe.wait_ge(b_tt, 2 * b + h + 1)
                await_(pe, b_lgs, 2 * b + h)
                for t in range(TU):
                    at = (h * TU + t) * E
                    last = nc.tensor.matmul(bl[:, at:at + E], tt[:, h, t * P:(t + 1) * P], g_c[:, :],
                                            start=True, stop=True)
                last.then_inc(b_logit, 1)

            def transpose_logits(b):
                pe.wait_ge(b_lgs, 2 * b + 2)
                await_(pe, b_exp, b)
                for h in range(2):
                    for q in range(2):
                        at = (2 * h + q) * P
                        last = nc.tensor.transpose(blt[:, at:at + P], lgs[:, h, 2 * q * E:(2 * q + 2) * E],
                                                   ident[:, :])
                last.then_inc(b_ltp, 1)

            def step(b, par, tri=False, resident=False):
                if live(b):
                    transpose_x2(b, 0)
                if tri:
                    triangle(b + CB, par, 0, resident)
                if live(b):
                    transpose_x2(b, 1)
                if live(b - 2):
                    transpose_logits(b - 2)
                if live(b):
                    gate(b, 0)
                if tri:
                    triangle(b + CB, par, 1, resident)
                if live(b - 1):
                    transpose_t(b - 1, 1 - par, 0)
                if live(b):
                    transpose_on(b, 0)
                    gate(b, 1)
                if live(b - 1):
                    transpose_t(b - 1, 1 - par, 1)
                if live(b):
                    transpose_on(b, 1)
                if live(b - 1):
                    logits(b - 1, 0)
                if live(b):
                    project_out(b, 0)
                if live(b - 1):
                    logits(b - 1, 1)
                if live(b):
                    project_out(b, 1)

            pe.wait_ge(a_side, 8 * NB)
            pe.wait_ge(b_resfirst, 64)
            for eb in range(2):
                for h in range(2):
                    triangle(eb, eb, h, False)
            with pe.Fori(1, CB // 2) as eb_2:
                for par in range(2):
                    for h in range(2):
                        triangle(2 * eb_2 + par, par, h, False)
            for b in range(4):
                step(b, b % 2, True)
            for lo, hi, tri_on, resident in [(4, 32, True, False), (32, 48, True, True), (48, 80, True, False),
                                             (80, 96, True, True), (96, 128, True, False),
                                             (128, NB - 2, False, False)]:
                with pe.Fori(lo // 2, hi // 2) as b_2:
                    for par in range(2):
                        step(2 * b_2 + par, par, tri_on, resident)
            for b in range(NB - 2, NB + 2):
                step(b, b % 2)

            pe.wait_ge(c_bias, 32)
            for c in range(HC):
                nc.tensor.transpose(bank[0][:, c * E:(c + 1) * E], ring32[0:E, c * P:(c + 1) * P], ident[0:E, 0:E])
            nc.tensor.transpose(bank[1][:, 0:E], ring32[0:E, HF:HF + D], ident[0:E, 0:E]).then_inc(c_btp, 1)
            pe.wait_ge(c_v, V_DIAG)
            pe.wait_ge(c_iota, 2)
            nc.tensor.matmul(bank[2][:, :], ones[0:E, 0:P], diag[0:E, :], start=True, stop=True).then_inc(c_row, 1)
            for s in range(4):
                pe.wait_ge(c_v, V_U + s)
                last = nc.tensor.matmul(bank[3][:, 0:E], u_rows[:, s, :], dtop[:, s, :], start=(s == 0), stop=(s == 3))
            last.then_inc(c_pooled, 1)
            pe.wait_ge(c_v, V_PT)

            def layer1(r, k):
                n = 4 * r + k
                await_(pe, c_hb, n)
                for e in range(XG):
                    for c in range(HC):
                        last = nc.tensor.matmul(bank[4][:, c * XG + e:c * XG + e + 1],
                                                experts[:, k * XG + e, 0, c * P:(c + 1) * P],
                                                pooled_t[:, n * XG + e:n * XG + e + 1], start=True, stop=True)
                last.then_inc(c_h, 1)

            def layer2(r, k):
                n = 4 * r + k
                pe.wait_ge(c_gelu, n + 1)
                for e in range(XG):
                    for c in range(HC):
                        last = nc.tensor.matmul(bank[5][:, n * XG + e:n * XG + e + 1],
                                                experts[:, k * XG + e, 1, c * P:(c + 1) * P],
                                                hid[:, n % 2, c * XG + e:c * XG + e + 1],
                                                start=(c == 0), stop=(c == HC - 1))
                last.then_inc(c_o, 1)

            pe.wait_ge(c_early, 3 * XG * 32)
            layer1(0, 0)
            for n in range(1, NXG):
                if n >= 3:
                    pe.wait_ge(c_w[n % 4], XG * 32 * (n // 4 if n % 4 < 3 else n // 4 + 1))
                layer1(n // 4, n % 4)
                layer2((n - 1) // 4, (n - 1) % 4)
            layer2((NXG - 1) // 4, (NXG - 1) % 4)
            pe.wait_ge(c_v, V_OT)
            nc.tensor.transpose(bank[6][0:E, 0:D], out_t[:, :], ident[:, :]).then_inc(c_otp, 1)
            pe.wait_ge(c_v, V_OE)
            for s in range(4):
                last = nc.tensor.matmul(bank[7][:, s * D:(s + 1) * D], share[0:E, s * P:(s + 1) * P], out_e[0:E, :],
                                        start=True, stop=True)
            last.then_inc(c_delta, 1)

        @block.scalar
        def _(act):
            nw, nb_, ow, ob = (cols[:, n:n + 1] for n in range(4))

            def out_of_x(u, h):
                act.wait_ge(a_tp, u + 1)
                await_(act, a_lr, 4 * (u - 1))
                nc.scalar.activation(xnt[:, h, :], bank[h][:, :], ACT.Identity, bias=nb_, scale=nw
                                     ).then_inc(a_xn, 1)

            def sigmoids(u, h):
                for j in range(2):
                    for t in range(2):
                        act.wait_ge(a_lr, 4 * u + 2 * j + t + 1)
                        await_(act, a_side, 4 * (u - 1) + 2 * j + t + 1)
                        nc.scalar.activation(sig[:, j, t, :], bank[2 + 2 * j + t][:, 2 * D:4 * D], ACT.Sigmoid
                                             ).then_inc(a_sig, 1)

            act.wait_ge(s_wload, 16 * 14)
            act.wait_ge(s_wcopy, 17)
            out_of_x(0, 0)
            for b in range(2):
                out_of_x(2 * b + 1, 1)
                sigmoids(2 * b, 0)
                out_of_x(2 * b + 2, 0)
                sigmoids(2 * b + 1, 1)
            with act.Fori(2, NB - 1, 1) as b:
                out_of_x(2 * b + 1, 1)
                sigmoids(2 * b, 0)
                out_of_x(2 * b + 2, 0)
                sigmoids(2 * b + 1, 1)
            out_of_x(2 * NB - 1, 1)
            sigmoids(2 * NB - 2, 0)
            sigmoids(2 * NB - 1, 1)

            bx, bg, be, bo, blt = bank[0], bank[1:3], bank[3], bank[4], bank[7]

            def out_of_triangle(b, h, reused):
                eb = b + CB
                act.wait_ge(b_tri, 2 * eb + h + 1)
                if reused:
                    act.wait_ge(b_on, CB * (b // CB))
                nc.scalar.activation(
                    tri[:, ds((eb // CB + 1) % 2, 1), :, ds((eb % CB) * TB + h * TU, TU)].rearrange(
                        "j o i d -> j (o i) d"),
                    be[:, :].rearrange("j (d i) -> j i d", d=TU), ACT.Copy).then_inc(b_triout, 1)

            def norm_o1(b):
                act.wait_ge(b_ost1, b + 1)
                await_(act, b_otp, 2 * b)
                for t in range(TU):
                    n = TU + t
                    last = nc.scalar.activation(
                        on[:, 1, t * D:(t + 1) * D],
                        tri[:, ds((b // CB + 1) % 2, 1), ds((b % CB) * TB + n, 1), :].rearrange(
                            "j o i d -> j (o i d)"),
                        ACT.Identity, bias=ost[:, 2, n:n + 1], scale=ost[:, 1, n:n + 1])
                last.then_inc(b_on1, 1)

            def out_of_x2(b, h):
                act.wait_ge(b_xtp, 2 * b + h + 1)
                await_(act, b_gate, 2 * (b - 1) + h + 1)
                nc.scalar.activation(xnt[:, h, :], bx[:, :], ACT.Identity, bias=nb_, scale=nw).then_inc(b_xn, 1)

            def gate_tanh(b, h):
                act.wait_ge(b_gate, 2 * b + h + 1)
                nc.scalar.activation(bg[h][:, :], bg[h][:, :], ACT.Tanh, scale=0.5).then_inc(b_tanh, 1)

            def out_of_on(b, h):
                act.wait_ge(b_otp, 2 * b + h + 1)
                await_(act, b_y, 2 * (b - 1) + h + 1)
                nc.scalar.activation(gated[:, h, :], bo[:, :], ACT.Identity, bias=ob, scale=ow).then_inc(b_onw, 1)

            def out_of_t(b, h):
                act.wait_ge(b_ttp, 2 * b + h + 1)
                await_(act, b_logit, 2 * (b - 1) + h + 1)
                nc.scalar.activation(tt[:, h, :], bx[:, :], ACT.Copy).then_inc(b_tt, 1)

            def exps(b):
                act.wait_ge(b_negm, b + 1)
                nc.scalar.activation(blt[:, :], blt[:, :], ACT.Exp, bias=negm[:, :],
                                     accum_out=csum[:, ds(b, 1)]).then_inc(b_exp, 1)

            def step(b, tri_on=False, reused=False):
                if live(b):
                    out_of_x2(b, 0)
                if tri_on:
                    out_of_triangle(b, 0, reused)
                if live(b):
                    out_of_x2(b, 1)
                    norm_o1(b)
                    gate_tanh(b, 0)
                if tri_on:
                    out_of_triangle(b, 1, reused)
                if live(b - 1):
                    out_of_t(b - 1, 0)
                if live(b):
                    out_of_on(b, 0)
                    gate_tanh(b, 1)
                if live(b - 1):
                    out_of_t(b - 1, 1)
                if live(b):
                    out_of_on(b, 1)
                if live(b - 2):
                    exps(b - 2)

            nc.scalar.activation(csum[:, 0:1], mhalf[:, 0:1], ACT.Exp)
            act.wait_ge(a_store, 32 * NCH)
            with act.Fori(0, CB, 1) as eb0:
                for h in range(2):
                    act.wait_ge(b_tri, 2 * eb0 + h + 1)
                    nc.scalar.activation(tri[:, 1, :, ds(eb0 * TB + h * TU, TU)],
                                         be[:, :].rearrange("j (d i) -> j i d", d=TU), ACT.Copy
                                         ).then_inc(b_triout, 1)
            for b in range(4):
                step(b, True)
            for lo, hi, tri_on, reused in [(4, CB, True, False), (CB, NB - CB, True, True),
                                           (NB - CB, NB, False, False)]:
                with act.Fori(lo, hi, 1) as b:
                    step(b, tri_on, reused)
            for b in range(NB, NB + 2):
                step(b)

            act.wait_ge(c_v, V_TOP)
            nc.scalar.activation(wexp[:, :], cand[:, :, 0], ACT.Exp, bias=negtop[:, :]).then_inc(c_act, 1)
            act.wait_ge(c_v, V_M2)
            nc.scalar.activation(hm[0:E, :], both[0:E, :, 16], ACT.Exp, bias=neg2[0:E, :]).then_inc(c_act, 1)
            nc.scalar.activation(ev[0:E, :], v8[0:E, :], ACT.Exp, bias=neg2[0:E, :]).then_inc(c_act, 1)

            def gelus(n, par):
                act.wait_ge(c_hb, n + 1)
                await_(act, c_o, n - 1)
                nc.scalar.activation(hid[:, par, :], hpre[:, par, :], ACT.Gelu).then_inc(c_gelu, 1)

            gelus(0, 0)
            gelus(1, 1)
            with act.Fori(1, NXG // 2) as n_2:
                for par in range(2):
                    gelus(2 * n_2 + par, par)

        @block.vector
        def _(dve):
            dests = [w_lr[:, n * D:(n + 1) * D] for n in range(4)] + [w_og[:, :]]
            for n in range(15):
                dve.wait_ge(s_wt, n + 1)
                src = bank[n % 2][:, 0:P]
                if n < 5:
                    nc.vector.tensor_copy(dests[n], src).then_inc(s_wcopy, 1)
                elif n == 5:
                    nc.vector.tensor_scalar(w_o[:, :], src, 0.5, None, ALU.mult).then_inc(s_wcopy, 1)
                else:
                    m = n - 6
                    nc.vector.tensor_copy(mask_t[:, m % NBLK, (m // NBLK) * P:(m // NBLK + 1) * P], src
                                          ).then_inc(s_wcopy, 1)
                if n == 5:
                    nc.vector.reduce_sum(negm[0:E, :], wraw[0:E, 6, :], axis=AX.X).then_inc(s_gmean, 1)
                    dve.wait_ge(s_gmean, 1)
                    nc.vector.tensor_scalar(tmp[0:E, 0, 0:1], negm[0:E, :], 1.0 / D, None, ALU.mult
                                            ).then_inc(s_gmean, 1)
                    dve.wait_ge(s_gmean, 2)
                    nc.vector.tensor_scalar(wraw[0:E, 7, :], wraw[0:E, 6, :], tmp[0:E, 0, 0:1], None,
                                            ALU.subtract).then_inc(s_gcen, 1)
            dve.wait_ge(s_wt, 16)
            nc.vector.tensor_copy(g_c[:, :], bank[1][:, 0:E]).then_inc(s_wcopy, 2)

            def moments(src, b, dst, s_bn, s_1, s_2, s_out):
                for t in range(TB):
                    last = nc.vector.bn_stats(bst[:, t, :], src(t))
                last.then_inc(s_bn, 1)
                dve.wait_ge(s_bn, b + 1)
                nc.vector.tensor_tensor(tmp[:, 0, :], bst[:, :, 1], bst[:, :, 4], ALU.subtract).then_inc(s_1, 1)
                nc.vector.tensor_tensor(dst[:, 0, :], bst[:, :, 1], bst[:, :, 4], ALU.add)
                nc.vector.tensor_tensor(tmp[:, 1, :], bst[:, :, 2], bst[:, :, 5], ALU.add)
                dve.wait_ge(s_1, b + 1)
                nc.vector.scalar_tensor_tensor(tmp[:, 2, :], tmp[:, 0, :], D / 4.0, tmp[:, 0, :], ALU.mult, ALU.mult
                                               ).then_inc(s_2, 1)
                dve.wait_ge(s_2, b + 1)
                nc.vector.tensor_tensor(dst[:, 1, :], tmp[:, 1, :], tmp[:, 2, :], ALU.add).then_inc(s_out, 1)

            def stats_x(b, slot):
                par = slot % 2
                dve.wait_ge(a_x[slot], 16 * (b // 4) + 16)
                await_(dve, a_pow, b - 1)
                moments(lambda t: x_slots[slot][:, t, :], b, sm[:, par, :, :], a_bn, a_s1, a_s2, a_sm)

            def stage_sides(b, stored):
                if stored:
                    dve.wait_ge(a_store, 32 * ((b - CB // 2) // CB))
                c = b // CB
                for n in range(TB):
                    dve.wait_ge(a_sig, TB * b + n + 1)
                    i = (b % RB) * TB + n
                    il = (b % CB) * TB + n
                    nc.vector.scalar_tensor_tensor(
                        stage[:, ds((c + 1) % 2, 1), :, :, ds(il, 1)].rearrange("k o s d i -> k (o s) (d i)"),
                        bank[2 + n % 4][:, 0:2 * D].rearrange("k (s d) -> k s d", s=2),
                        mask_t[:, ds(b // RB, 1), ds(i, 1)].rearrange("k o i -> k (o i)"),
                        sig[:, (n // 2) % 2, n % 2, :].rearrange("k (s d) -> k s d", s=2),
                        ALU.mult, ALU.mult).then_inc(a_side, 1)

            dve.wait_ge(s_wcopy, 17)
            stats_x(0, 0)
            stats_x(1, 1)
            for b in range(4):
                stats_x(b + 2, (b + 2) % 4)
                stage_sides(b, False)
            for lo, hi, stored in [(4, 24, False), (24, NB - 4, True)]:
                with dve.Fori(lo // 4, hi // 4) as q:
                    for k in range(4):
                        stats_x(4 * q + (k + 2), (k + 2) % 4)
                        stage_sides(4 * q + k, stored)
            for b in range(NB - 4, NB):
                if b + 2 < NB:
                    stats_x(b + 2, (b + 2) % 4)
                stage_sides(b, True)

            bg, by, bl, blt = bank[1:3], bank[5], bank[6], bank[7]

            def maxima(b):
                dve.wait_ge(b_ltp, b + 1)
                pass_on(dve, s_dve)
                nc.vector.max(m8[:, :], blt[:, :]).then_inc(b_m8, 1)
                dve.wait_ge(b_m8, b + 1)
                nc.vector.tensor_copy(cand[:, ds(b, 1), :], m8[:, :].rearrange("p (o k) -> p o k", o=1))
                nc.vector.max_index(i8[:, :], m8[:, :], blt[:, :]).then_inc(b_i8, 1)
                await_(dve, b_exp, b)
                nc.vector.tensor_scalar(negm[:, :], m8[:, 0:1], -1.0, None, ALU.mult).then_inc(b_negm, 1)
                dve.wait_ge(b_i8, b + 1)
                nc.vector.tensor_copy(cidx[:, ds(b, 1), :], i8[:, :].rearrange("p (o k) -> p o k", o=1)
                                      ).then_inc(b_keep, 1)

            def stats_t(b, par):
                dve.wait_ge(b_t, 2 * b + 2)
                moments(lambda t: tout[:, par, t, :], b, smt, b_bnt, b_t1, b_t2, b_smt)

            def gates(b, h):
                dve.wait_ge(b_tanh, 2 * b + h + 1)
                dve.wait_ge(b_onw, 2 * b + h + 1)
                nc.vector.scalar_tensor_tensor(gated[:, h, :], bg[h][:, :], 1.0, gated[:, h, :], ALU.add, ALU.mult
                                               ).then_inc(b_gated, 1)

            def scale_logits(b, h):
                dve.wait_ge(b_logit, 2 * b + h + 1)
                dve.wait_ge(b_rst, b + 1)
                await_(dve, b_ltp, b)
                nc.vector.tensor_tensor(
                    lgs[:, h, :].rearrange("p (t e) -> p t e", t=TU),
                    bl[:, h * TU * E:(h + 1) * TU * E].rearrange("p (t e) -> p t e", t=TU),
                    tst[:, 1, h * TU:(h + 1) * TU].unsqueeze(2).broadcast_to([P, TU, E]), ALU.mult
                ).then_inc(b_lgs, 1)

            def residual(b, par, h):
                dve.wait_ge(b_y, 2 * b + h + 1)
                if h == 0:
                    await_(dve, b_store[par], 16 * (b // 2))
                await_(dve, b_ttp, 2 * (b - 2) + h + 1)
                nc.vector.tensor_tensor(tout[:, par, h * TU:(h + 1) * TU, :],
                                        by[:, :].rearrange("p (t d) -> p t d", t=TU),
                                        xin[:, par, h * TU:(h + 1) * TU, :], ALU.add).then_inc(b_t, 1)

            def tri_tile(b, t):
                return tri[:, ds((b // CB + 1) % 2, 1), ds((b % CB) * TB + t, 1), :].rearrange("j o i d -> j (o i d)")

            def stats_o(b):
                dve.wait_ge(b_triout, 2 * CB * (b // CB) + 2 * CB)
                moments(lambda t: tri_tile(b, t), b, smo, b_bno, b_o1, b_o2, b_smo)

            def norm_o(b):
                dve.wait_ge(b_ost, b + 1)
                await_(dve, b_otp, 2 * (b - 1) + 1)
                for t in range(TU):
                    last = nc.vector.tensor_scalar(on[:, 0, t * D:(t + 1) * D], tri_tile(b, t),
                                                   ost[:, 0, t:t + 1], ost[:, 1, t:t + 1], ALU.add, ALU.mult)
                last.then_inc(b_on, 1)

            def step(b, par):
                if live(b - 1):
                    stats_t(b - 1, 1 - par)
                if live(b + 1):
                    stats_o(b + 1)
                if live(b):
                    gates(b, 0)
                    gates(b, 1)
                if live(b - 2):
                    maxima(b - 2)
                if live(b - 1):
                    scale_logits(b - 1, 0)
                if live(b):
                    residual(b, par, 0)
                if live(b - 1):
                    scale_logits(b - 1, 1)
                if live(b):
                    residual(b, par, 1)
                if live(b + 1):
                    norm_o(b + 1)

            stats_o(0)
            norm_o(0)
            for b in range(4):
                step(b, b % 2)
            with dve.Fori(2, NB // 2 - 1) as b_2:
                step(2 * b_2, 0)
                step(2 * b_2 + 1, 1)
            for b in range(NB - 2, NB + 2):
                step(b, b % 2)

            count = [0]

            def done(ins):
                count[0] += 1
                ins.then_inc(c_v, 1)
                dve.wait_ge(c_v, count[0])

            def mark(value):
                assert count[0] == value, (count[0], value)

            dve.wait_ge(b_exp, NB)
            for par in range(2):
                dve.wait_ge(b_store[par], 16 * NB // 2)
            dve.wait_ge(b_keep, NB)
            cflat = cand[:, :, :].rearrange("p b k -> p (b k)")
            iflat = cidx[:, :, :].rearrange("p b k -> p (b k)")
            done(nc.vector.memset(par384[0:E, :], 0.0))
            done(nc.vector.memset(par384[E:2 * E, :], float(N)))
            done(nc.vector.tensor_scalar(cflat, cflat, gb[:, :], None, ALU.add))
            done(nc.vector.max(both[:, 0, 0:8], cflat))
            done(nc.vector.tensor_scalar(negtop[:, :], both[:, 0, 0:1], -1.0, None, ALU.mult))
            mark(V_TOP)
            done(nc.vector.max_index(pos_i[:, :], both[:, 0, 0:8], cflat))
            done(nc.vector.tensor_copy(pos_f[:, :], pos_i[:, :]))
            dve.wait_ge(c_iota, 1)
            done(nc.vector.tensor_copy(iota_f, iota_i))
            for k in range(K):
                last = nc.vector.scalar_tensor_tensor(pick, iota_f, pos_f[:, k:k + 1], iflat, ALU.is_equal, ALU.mult,
                                                      accum_out=raw[:, k:k + 1])
                if k < K - 1:
                    done(last)
            done(last)
            done(nc.vector.tensor_copy(raw_i[:, :], raw[:, :]))
            done(nc.vector.tensor_scalar(bi[:, :], pos_i[:, :], 3, None, ALU.logical_shift_right))
            done(nc.vector.tensor_scalar(qi[:, :], raw_i[:, :], 7, None, ALU.logical_shift_right))
            done(nc.vector.tensor_copy(bf[:, :], bi[:, :]))
            done(nc.vector.tensor_copy(qf[:, :], qi[:, :]))
            done(nc.vector.scalar_tensor_tensor(tok[:, :], qf[:, :], float(2 * N - P), raw[:, :], ALU.mult, ALU.add))
            done(nc.vector.scalar_tensor_tensor(tok[:, :], bf[:, :], float(TB * N), tok[:, :], ALU.mult, ALU.add))
            dve.wait_ge(c_iota, 2)
            done(nc.vector.tensor_scalar(tok[:, :], tok[:, :], par384[:, :], None, ALU.add))
            for m in range(1, NBLK):
                done(nc.vector.tensor_scalar(qf[:, :], bf[:, :], float(m * RB), float(P - S), ALU.is_ge, ALU.mult))
                done(nc.vector.tensor_tensor(both[:, 0, 8:16] if m == NBLK - 1 else tok[:, :], tok[:, :], qf[:, :],
                                             ALU.add))
            done(nc.vector.tensor_copy(both[:, 0, 16:17], both[:, 0, 0:1]))
            dve.wait_ge(c_act, 1)
            done(nc.vector.tensor_tensor(wexp[:, :], wexp[:, :], csum[:, :], ALU.mult))
            done(nc.vector.reduce_sum(both[:, 0, 17:18], wexp[:, :], axis=AX.X))
            mark(V_FIN)
            dve.wait_ge(c_half, 16)
            done(nc.vector.tensor_copy(v16[0:E, :, :], both[0:E, :, 0:8]))
            done(nc.vector.tensor_copy(t16[0:E, :, :], both[0:E, :, 8:16]))
            v16f = v16[0:E, :, :].rearrange("p s k -> p (s k)")
            t16f = t16[0:E, :, :].rearrange("p s k -> p (s k)")
            done(nc.vector.max(v8[0:E, :], v16f))
            done(nc.vector.tensor_scalar(neg2[0:E, :], v8[0:E, 0:1], -1.0, None, ALU.mult))
            mark(V_M2)
            done(nc.vector.max_index(pos_i[0:E, :], v8[0:E, :], v16f))
            done(nc.vector.tensor_copy(pos_f[0:E, :], pos_i[0:E, :]))
            for k in range(K):
                done(nc.vector.scalar_tensor_tensor(pick[0:E, 0:16], iota_f[0:E, 0:16], pos_f[0:E, k:k + 1], t16f,
                                                    ALU.is_equal, ALU.mult, accum_out=kv[0:E, 0, k:k + 1]))
            dve.wait_ge(c_act, 3)
            done(nc.vector.tensor_tensor(hm[0:E, :], hm[0:E, :], both[0:E, :, 17], ALU.mult))
            done(nc.vector.reduce_sum(den[0:E, :], hm[0:E, :], axis=AX.X))
            done(nc.vector.reciprocal(den[0:E, :], den[0:E, :]))
            done(nc.vector.tensor_scalar(kv[0:E, 1, :], ev[0:E, :], den[0:E, :], None, ALU.mult))
            mark(V_KV)
            done(nc.vector.tensor_tensor(
                diag[0:E, :].rearrange("p (k e) -> p k e", k=K),
                ident[0:E, 0:E].unsqueeze(1).broadcast_to([E, K, E]),
                kv[0:E, 0, :].unsqueeze(2).broadcast_to([E, K, E]), ALU.mult))
            mark(V_DIAG)
            dve.wait_ge(c_kv, 16)
            for half in range(2):
                sl = slice(half * E, (half + 1) * E)
                done(nc.vector.tensor_copy(sel[sl, :, :],
                                           kv[sl, :, :].rearrange("p v (s h) -> p v s h", h=2)[:, :, :, half]))
            done(nc.vector.tensor_copy(idx_i[:, :], sel[:, 0, :]))
            mark(V_IDX)
            dve.wait_ge(c_row, 1)
            done(nc.vector.tensor_copy(idx_row[:, :], bank[2][:, :]))
            done(nc.vector.tensor_scalar(share[0:E, :], idx_row[0:E, :], kv[0:E, 0, 0:1], kv[0:E, 1, 0:1],
                                         ALU.is_equal, ALU.mult))
            for k in range(1, K):
                done(nc.vector.tensor_scalar(part[0:E, :], idx_row[0:E, :], kv[0:E, 0, k:k + 1], kv[0:E, 1, k:k + 1],
                                             ALU.is_equal, ALU.mult))
                done(nc.vector.tensor_tensor(share[0:E, :], share[0:E, :], part[0:E, :], ALU.add))
            done(nc.vector.tensor_copy(id2[0:E, :], ident[0:E, 0:E]))
            done(nc.vector.tensor_copy(id2[E:2 * E, :], ident[E:2 * E, E:2 * E]))
            for s in range(4):
                done(nc.vector.tensor_scalar(dtop[:, s, :], id2[:, :], sel[:, 1, s:s + 1], None, ALU.mult))
            dve.wait_ge(c_gather, 64)
            for s in range(4):
                done(nc.vector.bn_stats(bst[:, s, :], t_rows[:, s, :]))
            for s in range(4):
                done(nc.vector.bn_aggr(mv4[:, s, :], bst[:, s, :]))
            mark(V_VAR)
            dve.wait_ge(c_pool, 2)
            for s in range(4):
                done(nc.vector.tensor_scalar(u_rows[:, s, :], t_rows[:, s, :], mv4[:, s, 0:1], rst4[:, s:s + 1],
                                             ALU.subtract, ALU.mult))
                mark(V_U + s)
            dve.wait_ge(c_btp, 1)
            done(nc.vector.tensor_copy(b1_t, bank[0][:, 0:HC * E]))
            done(nc.vector.tensor_copy(b2_t, bank[1][:, 0:E]))
            dve.wait_ge(c_iota, 3)
            dve.wait_ge(c_pooled, 1)
            done(nc.vector.tensor_copy(pooled_t[:, :], bank[3][:, 0:E]))
            mark(V_PT)
            for s in range(4):
                done(nc.vector.scalar_tensor_tensor(part[:, :], idx_row[:, :], sel[:, 0, s:s + 1], earlier[:, s, :],
                                                    ALU.is_equal, ALU.mult, accum_out=dup[:, s:s + 1]))
            done(nc.vector.scalar_tensor_tensor(dup[:, :], dup[:, :], float(S), sel[:, 0, :], ALU.mult, ALU.add))
            done(nc.vector.tensor_copy(idx_w[:, :], dup[:, :]))

            def hidden(n, par):
                dve.wait_ge(c_h, n + 1)
                await_(dve, c_gelu, n - 1)
                nc.vector.tensor_tensor(
                    hpre[:, par, :].rearrange("p (c e) -> p c e", c=HC),
                    bank[4][:, 0:HC * XG].rearrange("p (c e) -> p c e", c=HC),
                    b1_t.rearrange("p (c e) -> p c e", c=HC)[:, :, ds(n * XG, XG)], ALU.add).then_inc(c_hb, 1)

            hidden(0, 0)
            hidden(1, 1)
            with dve.Fori(1, NXG // 2) as n_2:
                for par in range(2):
                    hidden(2 * n_2 + par, par)
            dve.wait_ge(c_o, NXG)
            done(nc.vector.tensor_tensor(out_t[:, :], bank[5][:, 0:E], b2_t, ALU.add))
            mark(V_OT)
            dve.wait_ge(c_otp, 1)
            done(nc.vector.tensor_copy(out_e[0:E, :], bank[6][0:E, 0:D]))
            mark(V_OE)
            dve.wait_ge(c_delta, 1)
            done(nc.vector.tensor_tensor(new_rows[:, :, :], bank[7][:, :].rearrange("p (s d) -> p s d", s=4),
                                         t_rows[:, :, :], ALU.add))
            mark(V_NEW)


_INS = ['x', 'L0_conv_mask', 'L0_conv_norm_w', 'L0_conv_norm_b', 'L0_conv_W_left', 'L0_conv_W_right',
        'L0_conv_W_left_gate', 'L0_conv_W_right_gate', 'L0_conv_W_out_gate', 'L0_conv_out_norm_w',
        'L0_conv_out_norm_b', 'L0_conv_W_out', 'L0_ffn_gate_w', 'L0_ffn_gate_b', 'L0_ffn_weight1',
        'L0_ffn_weight2']


def kernel(**inputs):
    import numpy as _np
    import concourse.bacc as _bacc
    from concourse import mybir as _mybir
    from concourse.bass_utils import run_bass_kernel_spmd as _run

    nc = _bacc.Bacc("TRN2", target_bir_lowering=False, num_devices=1)
    arrays, args = {}, []
    for name in _INS:
        a = _np.ascontiguousarray(inputs[name])
        arrays[f"in_{name}_dram"] = a
        args.append(nc.dram_tensor(f"in_{name}_dram", a.shape, _mybir.dt.from_np(a.dtype), kind="ExternalInput").ap())
    shape = inputs["x"].shape
    args.append(nc.dram_tensor("out_0_dram", shape, _mybir.dt.float32, kind="ExternalOutput").ap())
    metaformer_layer_kernel(nc, *args)
    r = _run(nc, [arrays], core_ids=[0])
    return r.results[0]["out_0_dram"]
```

```python
import concourse.bass as bass
from concourse import mybir
from contextlib import ExitStack


def metaformer_layer_kernel(
    nc: bass.Bass,
    x: bass.AP,
    mask: bass.AP,
    norm_w: bass.AP,
    norm_b: bass.AP,
    W_left: bass.AP,
    W_right: bass.AP,
    W_left_gate: bass.AP,
    W_right_gate: bass.AP,
    W_out_gate: bass.AP,
    out_norm_w: bass.AP,
    out_norm_b: bass.AP,
    W_out: bass.AP,
    gate_w: bass.AP,
    gate_b: bass.AP,
    weight1: bass.AP,
    weight2: bass.AP,
    out: bass.AP,
):
    fp32 = mybir.dt.float32
    bf16 = mybir.dt.bfloat16
    u32 = mybir.dt.uint32
    i32 = mybir.dt.int32
    ALU = mybir.AluOpType
    ACT = mybir.ActivationFunctionType
    AX = mybir.AxisListType
    ds = bass.ds

    P = 128
    N = x.shape[1]
    D = x.shape[3]
    E = gate_w.shape[0]
    HF = weight1.shape[2]
    K = 8
    S = N * N
    NBLK = N // P
    TB = 8
    TU = TB // 2
    RB = N // TB
    NB = NBLK * RB
    CB = P // TB
    NCH = NB // CB
    EPS_C = 1e-6
    EPS = 1e-5
    HC = HF // P
    XG = 8
    EG = E // 2
    DVE_TILES = 3

    x3 = x[0]
    mask2 = mask[0]
    out3 = out[0]
    rows = out[0].rearrange("i j d -> (i j) d")

    ctx = ExitStack()
    with ctx:
        def sb(name, shape, dt):
            return ctx.enter_context(nc.sbuf_tensor(name, shape, dt))

        def pb(name, shape, dt):
            return ctx.enter_context(nc.psum_tensor(name, shape, dt))

        def sem(name):
            return ctx.enter_context(nc.semaphore(name))

        sides = nc.dram_tensor("sides", (2, NBLK, NBLK, P, D * P), bf16, kind="Internal").ap()

        arena = sb("arena", [P, 4 * D * P], bf16)
        stage = arena[:, :].rearrange("k (c s d i) -> k c s d i", c=2, s=2, d=D)
        right_res = arena[:, 0:2 * D * P].rearrange("k (t d j) -> k t d j", t=2, d=D)
        tri = arena[:, 2 * D * P:4 * D * P].rearrange("j (c i d) -> j c i d", c=2, i=P)
        experts = arena[:, :].bitcast(fp32).rearrange("p (e l h) -> p e l h", l=2, h=HF)
        ring = sb("ring", [P, 2 * 4 * TB * P], bf16)
        lr = ring[:, :].rearrange("k (s q d i) -> k s q d i", s=2, q=4, d=TB)
        ring32 = ring[:, :].bitcast(fp32)
        mask_t = ring32[:, 0:NBLK * N].rearrange("k (b i) -> k b i", b=NBLK)

        work = sb("work", [P, 2 * 2 * TB * D + 5 * TB * D + TB * E + 2 * NB * TB], fp32)
        at = [0]

        def piece(*shape):
            n = 1
            for v in shape:
                n *= v
            flat = work[:, at[0]:at[0] + n]
            at[0] += n
            names = "abc"[:len(shape)]
            return flat.rearrange(f"p ({' '.join(names)}) -> p {' '.join(names)}",
                                  **{k: v for k, v in zip(names, shape)})

        tout = piece(2, TB, D)
        xin = piece(2, TB, D)
        xh, xnt, on, gated, tt = (piece(2, TU * D) for _ in range(5))
        lgs = piece(2, TU * E)
        stats = piece(2, NB * TB)
        x_slots = [xin[:, 0, :, :], xin[:, 1, :, :]] + [
            v.rearrange("p h (t d) -> p (h t) d", d=D) for v in (on, gated)]
        sig = tout[:, 0, :, :].rearrange("p (j t) d -> p j (t d)", j=2).rearrange(
            "p j (t c) -> p j t c", t=2)
        w_lr = tt[:, 0, :]
        cand = sb("cand", [P, NB, K], fp32)
        cidx = sb("cidx", [P, NB, K], mybir.dt.uint16)
        csum = sb("csum", [P, NB], fp32)
        ident = sb("ident", [P, P], fp32)
        w_og = sb("w_og", [D, D], fp32)
        w_o = sb("w_o", [D, D], fp32)
        g_c = sb("g_c", [D, E], fp32)
        cols = sb("cols", [P, 4], fp32)
        gb = sb("gb", [P, 1], fp32)
        mhalf = sb("mhalf", [P, TB], fp32)
        bst = sb("bst", [P, 2 * TB, 6], fp32)
        tmp = sb("tmp", [P, 3, 2 * TB], fp32)
        sm = sb("sm", [P, 2, 2, TB], fp32)
        xst = sb("xst", [P, 2, 2, TB], fp32)
        sm2 = sb("sm2", [P, 2, 2 * TB], fp32)
        st2 = sb("st2", [P, 2, 3, 2 * TB], fp32)
        tst, ost = st2[:, :, :, 0:TB], st2[:, :, :, TB:2 * TB]
        m8 = sb("m8", [P, K], fp32)
        negm = sb("negm", [P, 1], fp32)
        i8 = sb("i8", [P, K], u32)
        wraw = xin[:, 0, :, :]

        used = [0]

        def carve(shape, dt=fp32):
            n = 1
            for v in shape:
                n *= v
            at = used[0]
            used[0] += n
            flat = work[:, at:at + n]
            if dt != fp32:
                flat = flat.bitcast(dt)
            if len(shape) == 2:
                return flat.rearrange("p (a b) -> p a b", a=shape[0])
            return flat

        iota_i, pick, iota_f = carve([NB * K], i32), carve([NB * K]), carve([NB * K])
        earlier = work[:, 0:4 * 4 * P].rearrange("p (s a) -> p s a", s=4)
        ones = carve([P])
        idx_row, share, part, diag = (carve([K * E]) for _ in range(4))
        t_rows, u_rows, new_rows = (carve([4, D]) for _ in range(3))
        dtop, id2 = carve([4, E]), carve([E])
        hid, hpre, out_e = carve([HF]), carve([HF]), carve([D])
        b1_rows, b2_rows = carve([HF]), carve([D])
        pooled_d = carve([2, EG * EG])
        hid_d = ring32.rearrange("p (c n) -> p c n", c=HC)
        wexp = carve([NB])
        both, kv, sel = carve([2, 18]), carve([2, K]), carve([2, 4])
        v16, t16 = carve([2, K]), carve([2, K])
        pos_i, raw_i, bi, qi = (carve([K], u32) for _ in range(4))
        pos_f, raw, bf, qf, tok, v8, ev = (carve([K]) for _ in range(7))
        idx_i, idx_w = carve([4], i32), carve([4], i32)
        mv4, rst4, dup = carve([4, 2]), carve([4]), carve([4])
        hm, den = carve([2]), carve([1])
        par384, negtop, neg2 = carve([1]), carve([1]), carve([1])
        V_TOP, V_FIN, V_M2, V_KV, V_DIAG, V_IDX = 5, 31, 35, 49, 50, 53
        V_PICKED, V_VAR, V_U, V_PT, V_OE, V_NEW = 16, 83, 84, 89, 96, 97

        bank = [pb(f"bank{i}", [P, 512], fp32) for i in range(8)]

        s_ident = sem("s_ident")
        s_const = sem("s_const")
        s_pool = sem("s_pool")
        s_dve = sem("s_dve")
        s_sp = sem("s_sp")
        s_wload = sem("s_wload")
        s_wt = sem("s_wt")
        s_wcopy = sem("s_wcopy")
        s_gmean = sem("s_gmean")
        s_gcen = sem("s_gcen")
        a_x = [sem(f"a_x{i}") for i in range(4)]
        a_bn = sem("a_bn")
        a_s1 = sem("a_s1")
        a_s2 = sem("a_s2")
        a_sm = sem("a_sm")
        a_arg = sem("a_arg")
        a_pow = sem("a_pow")
        a_keep = sem("a_keep")
        a_xh = sem("a_xh")
        a_tp = sem("a_tp")
        a_xn = sem("a_xn")
        a_lr = sem("a_lr")
        a_sig = sem("a_sig")
        a_side = sem("a_side")
        a_store = sem("a_store")
        a_last = [sem(f"a_last{side}") for side in range(2)]
        b_x = [[sem(f"b_x{i}{h}") for h in range(2)] for i in range(2)]
        b_lr = [sem(f"b_lr{i}") for i in range(2)]
        b_resfirst = sem("b_resfirst")
        b_res = [sem(f"b_res{i}") for i in range(2)]
        b_store = [sem(f"b_store{i}") for i in range(2)]
        b_xst = sem("b_xst")
        b_xh = sem("b_xh")
        b_xtp = sem("b_xtp")
        b_xn = sem("b_xn")
        b_gate = sem("b_gate")
        b_tanh = sem("b_tanh")
        b_tri = sem("b_tri")
        b_triout = sem("b_triout")
        b_bn = sem("b_bn")
        b_s1 = sem("b_s1")
        b_s2 = sem("b_s2")
        b_sm = sem("b_sm")
        b_arg = sem("b_arg")
        b_ost = sem("b_ost")
        b_ost1 = sem("b_ost1")
        b_on = sem("b_on")
        b_on0 = sem("b_on0")
        b_on1 = sem("b_on1")
        b_otp = sem("b_otp")
        b_onw = sem("b_onw")
        b_gated = sem("b_gated")
        b_y = sem("b_y")
        b_t = sem("b_t")
        b_rst = sem("b_rst")
        b_ttp = sem("b_ttp")
        b_tt = sem("b_tt")
        b_logit = sem("b_logit")
        b_lgs = sem("b_lgs")
        b_ltp = sem("b_ltp")
        b_m8 = sem("b_m8")
        b_negm = sem("b_negm")
        b_i8 = sem("b_i8")
        b_keep = sem("b_keep")
        b_exp = sem("b_exp")
        c_early = sem("c_early")
        c_w3 = sem("c_w3")
        c_w1 = [sem(f"c_w1{i}") for i in range(4)]
        c_w2 = [sem(f"c_w2{i}") for i in range(4)]
        c_l1 = sem("c_l1")
        c_l2 = sem("c_l2")
        c_zero = sem("c_zero")
        c_htp = sem("c_htp")
        c_hd = sem("c_hd")
        c_bias = sem("c_bias")
        c_iota = sem("c_iota")
        c_v = sem("c_v")
        c_act = sem("c_act")
        c_half = sem("c_half")
        c_kv = sem("c_kv")
        c_pool = sem("c_pool")
        c_row = sem("c_row")
        c_gather = sem("c_gather")
        c_pooled = sem("c_pooled")
        c_hb = sem("c_hb")
        c_gelu = sem("c_gelu")
        c_delta = sem("c_delta")
        c_scatter = sem("c_scatter")

        def live(n):
            return not isinstance(n, int) or 0 <= n < NB

        def await_(eng, s, v):
            if not isinstance(v, int) or v > 0:
                eng.wait_ge(s, v)

        def pass_on(eng, s):
            eng.sem_inc(s, 1)

        def rows_of(b):
            return ds((b % RB) * TB, TB)

        def cols_of(b):
            return ds((b // RB) * P, P)

        block = ctx.enter_context(nc.Block())

        @block.sync
        def _(sp):
            for n, w in enumerate([W_left, W_right, W_left_gate, W_right_gate, W_out_gate, W_out]):
                sp.dma_start(wraw[:, n, :], w).then_inc(s_wload, 16)
            sp.dma_start(wraw[0:E, 6, :], gate_w).then_inc(s_wload, 16)
            for n, w in enumerate([norm_w, norm_b, out_norm_w, out_norm_b]):
                sp.dma_start(cols[:, n:n + 1], w.rearrange("(d o) -> d o", o=1)).then_inc(s_wload, 16)
            for h in range(2):
                sp.dma_start(gb[h * E:(h + 1) * E, :], gate_b.rearrange("(d o) -> d o", o=1)).then_inc(s_wload, 16)
            sp.dma_start(tout[:, :, :, :].rearrange("p s t d -> p (s t d)")[:, 0:NBLK * N].rearrange(
                "p (b k) -> p b k", b=NBLK), mask2.rearrange("(b i) k -> i b k", b=NBLK)).then_inc(s_wload, 16)

            def load_x(b, slot):
                await_(sp, a_xh, 2 * (b - 4) + 2)
                sp.dma_start(x_slots[slot], x3[rows_of(b), cols_of(b), :].rearrange("i j d -> j i d")
                             ).then_inc(a_x[slot], 16)

            def load_xs(lo, hi):
                with sp.Fori(lo // 4, hi // 4) as q:
                    for slot in range(4):
                        load_x(4 * q + slot, slot)

            sp.wait_ge(s_wcopy, 17)
            for b in range(4):
                load_x(b, b)
            def store_side(c, side, quarter, stored):
                n = D * P // 4
                sp.dma_start(sides[ds(side, 1), c // NBLK, c % NBLK, :, quarter * n:(quarter + 1) * n
                                   ].rearrange("s k n -> k (s n)"),
                             stage[:, (c + 1) % 2, ds(side, 1), quarter * D // 4:(quarter + 1) * D // 4, :
                                   ].rearrange("k s d i -> k (s d i)")).then_inc(stored, 16)

            for c in range(NCH):
                load_xs(CB * c + 4, CB * c + 8)
                if c == 0:
                    load_xs(8, 16)
                else:
                    sp.wait_ge(a_side, P * c)
                    if c > 1:
                        sp.wait_ge(a_store, 8 * 16 * (c - 1))
                    with sp.Fori(0, 2, 1) as side:
                        for slot in range(4):
                            load_x(CB * c + 8 + 4 * side + slot, slot)
                            store_side(c - 1, side, slot, a_store)
                if c < NCH - 1:
                    load_xs(CB * c + 16, CB * c + 20)
            sp.wait_ge(a_store, 8 * 16 * (NCH - 1))
            for g in range(4):
                sp.dma_start(right_res[:, :, g * D // 4:(g + 1) * D // 4, :].rearrange("k t d j -> k t (d j)"),
                             sides[1, 0:2, 0, :, g * D * P // 4:(g + 1) * D * P // 4].rearrange("t k n -> k t n")
                             ).then_inc(b_resfirst, 16)
            sp.wait_ge(a_side, P * NCH)
            for quarter in range(4):
                store_side(NCH - 1, 1, quarter, a_last[1])

            def load_lr(eb, par, resident):
                c = eb // CB
                jb, ib = c // NBLK, c % NBLK
                at = (eb % CB) * TB * P
                await_(sp, b_tri, 2 * (eb - 2) + 2)
                sp.dma_start(lr[:, par, 0:3, :, :].rearrange("k q d i -> k q (d i)"),
                             sides[0, :, ds(ib, 1), :, ds(at, TB * P)].rearrange("t o k n -> k (t o) n")
                             ).then_inc(b_lr[par], 16)
                sp.dma_start(lr[:, par, 3, :, :].rearrange("k d i -> k (d i)"),
                             sides[1, 2, ds(jb, 1), :, ds(at, TB * P)].rearrange("o k n -> k (o n)")
                             ).then_inc(b_lr[par], 16)
                if resident:
                    sp.dma_start(right_res[:, :, ds((eb % CB) * TB, TB), :].rearrange("k t d j -> k t (d j)"),
                                 sides[1, 0:2, ds(jb, 1), :, ds(at, TB * P)].rearrange("t o k n -> k (t o) n")
                                 ).then_inc(b_res[par], 16)

            def load_x2(b, par):
                await_(sp, b_xh, 2 * (b - 2) + 2)
                pass_on(sp, s_sp)
                for h in range(2):
                    await_(sp, b_t, 2 * (b - 2) + h + 1)
                    pass_on(sp, s_sp)
                    sp.dma_start(xin[:, par, h * TU:(h + 1) * TU, :],
                                 x3[ds((b % RB) * TB + h * TU, TU), cols_of(b), :].rearrange("i j d -> j i d")
                                 ).then_inc(b_x[par][h], 16)

            def store_t(b, par):
                sp.wait_ge(b_t, 2 * b + 2)
                sp.dma_start(out3[rows_of(b), cols_of(b), :].rearrange("i j d -> j i d"), tout[:, par, :, :]
                             ).then_inc(b_store[par], 16)

            load_lr(0, 0, False)
            load_lr(1, 1, False)
            for quarter in range(4):
                store_side(NCH - 1, 0, quarter, a_last[0])
            load_x2(0, 0)
            load_x2(1, 1)
            with sp.Fori(1, CB // 2 + 1) as eb_2:
                for par in range(2):
                    load_lr(2 * eb_2 + par, par, False)
            load_lr(CB + 2, 0, False)
            sp.wait_ge(a_last[0], 64)
            sp.wait_ge(a_last[1], 64)
            LA = CB + 3

            def step(b, par, resident):
                load_x2(b + 2, par)
                load_lr(b + LA, 1 - par, resident)
                store_t(b, par)

            step(0, 0, False)
            for lo, hi, resident in [(1, 29, False), (29, 45, True), (45, 77, False), (77, 93, True),
                                     (93, NB - LA, False)]:
                with sp.Fori((lo - 1) // 2, (hi - 1) // 2) as b_2:
                    for k in range(2):
                        step(2 * b_2 + 1 + k, 1 - k, resident)
            for b in range(NB - LA, NB - CB):
                load_x2(b + 2, b % 2)
                store_t(b, b % 2)

            def load_layer1(e, slot, s_load):
                sp.dma_start(experts[:, ds(slot, 1), 0, :].rearrange("d e h -> d (e h)"),
                             weight1[ds(e, 1), 0:D, :].rearrange("e d h -> d (e h)")).then_inc(s_load, 16)

            def load_layer2(e, slot, s_load):
                sp.dma_start(experts[:, ds(slot, 1), 1, :].rearrange("p e (c o) -> p (e c) o", c=HC),
                             weight2[ds(e, 1), 0:HF, :].rearrange("e (c h) o -> h (e c) o", c=HC)
                             ).then_inc(s_load, 16)

            sp.wait_ge(b_tri, 2 * NB)
            sp.wait_ge(b_on, NB - CB)
            sp.wait_ge(b_on0, NB - CB)
            sp.wait_ge(b_on1, NB - CB)

            def early_experts(q):
                for k in range(3):
                    load_layer1(3 * q + k, 3 * q + k, c_early)
                    load_layer2(3 * q + k, 3 * q + k, c_early)

            with sp.Fori(0, CB // 2 - 1) as q:
                early_experts(q)
                for par in range(2):
                    b = 2 * q + NB - CB + par
                    load_x2(b + 2, par)
                    store_t(b, par)
            early_experts(CB // 2 - 1)
            store_t(NB - 2, 0)
            store_t(NB - 1, 1)
            sp.wait_ge(b_on, NB)
            sp.wait_ge(b_on0, NB)
            sp.wait_ge(b_on1, NB)
            with sp.Fori(0, XG) as e:
                load_layer1(3 * XG + e, 3 * XG + e, c_w3)
                load_layer2(3 * XG + e, 3 * XG + e, c_w3)
            sp.wait_ge(b_exp, NB)
            for par in range(2):
                sp.wait_ge(b_store[par], 16 * NB // 2)
            sp.dma_start(b1_rows[0:E, :], weight1[:, D, :]).then_inc(c_bias, 16)
            sp.dma_start(b2_rows[0:E, :], weight2[:, HF, :]).then_inc(c_bias, 16)
            sp.wait_ge(c_v, V_FIN)
            sp.dma_start(both[0:E, 1, :], both[E:2 * E, 0, :]).then_inc(c_half, 16)
            sp.wait_ge(c_v, V_KV)
            sp.dma_start(kv[E:2 * E, :, :], kv[0:E, :, :]).then_inc(c_kv, 16)
            for k in range(4):
                sp.wait_ge(c_l1, k + 1)
                with sp.Fori(0, XG) as e:
                    load_layer1(EG + k * XG + e, k * XG + e, c_w1[k])
            for k in range(4):
                sp.wait_ge(c_l2, k + 1)
                with sp.Fori(0, XG) as e:
                    load_layer2(EG + k * XG + e, k * XG + e, c_w2[k])
            sp.wait_ge(c_scatter, 64)

        @block.gpsimd
        def _(pool):
            nc.gpsimd.memset(ident[:, :], 0.0).then_inc(s_ident, 1)
            nc.gpsimd.memset(mhalf[:, :], -0.5).then_inc(s_const, 1)
            pool.wait_ge(s_ident, 1)
            nc.gpsimd.affine_select(out=ident[:, :], in_=ident[:, :], compare_op=ALU.not_equal, fill=1.0,
                                    base=0, pattern=[[-1, P]], channel_multiplier=1).then_inc(s_ident, 1)

            def norm_x(b, par, slot):
                pool.wait_ge(a_sm, b + 1)
                await_(pool, a_keep, b - 1)
                pass_on(pool, s_pool)
                nc.gpsimd.tensor_scalar(xst[:, par, 1, :], sm[:, par, 1, :], (1.0 + EPS) / D, EPS * EPS_C,
                                        ALU.mult, ALU.add).then_inc(a_arg, 1)
                nc.gpsimd.tensor_scalar(xst[:, par, 0, :], sm[:, par, 0, :], -0.5, 0.0,
                                        ALU.mult, ALU.add)
                pool.wait_ge(a_arg, b + 1)
                nc.gpsimd.tensor_tensor(xst[:, par, 1, :], xst[:, par, 1, :], mhalf[:, :], ALU.pow
                                        ).then_inc(a_pow, 1)
                pool.wait_ge(a_pow, b + 1)
                nc.gpsimd.tensor_copy(stats[:, :, ds(b * TB, TB)], xst[:, par, :, :]).then_inc(a_keep, 1)
                for h in range(2):
                    await_(pool, a_tp, 2 * (b - 1) + h + 1)
                    pass_on(pool, s_pool)
                    for t in range(TU):
                        n = h * TU + t
                        last = nc.gpsimd.tensor_scalar(xh[:, h, t * D:(t + 1) * D], x_slots[slot][:, n, :],
                                                       xst[:, par, 0, n:n + 1], xst[:, par, 1, n:n + 1],
                                                       ALU.add, ALU.mult)
                    last.then_inc(a_xh, 1)

            pool.wait_ge(s_const, 1)
            for b in range(4):
                norm_x(b, b % 2, b)
            with pool.Fori(1, NB // 4) as q:
                for slot in range(4):
                    norm_x(4 * q + slot, slot % 2, slot)

            pool.wait_ge(a_keep, NB)

            def norm_x2(b, par, h):
                if h == 0:
                    nc.gpsimd.tensor_copy(xst[:, par, :, :], stats[:, :, ds(b * TB, TB)]).then_inc(b_xst, 1)
                    pool.wait_ge(b_xst, b + 1)
                pool.wait_ge(b_x[par][h], 16 * (b // 2) + 16)
                if isinstance(b, int) and b == 0:
                    pool.wait_ge(a_tp, 2 * NB - 1 + h)
                else:
                    pool.wait_ge(b_xtp, 2 * (b - 1) + h + 1)
                pass_on(pool, s_pool)
                for t in range(TU):
                    n = h * TU + t
                    last = nc.gpsimd.tensor_scalar(xh[:, h, t * D:(t + 1) * D], xin[:, par, n, :],
                                                   xst[:, par, 0, n:n + 1], xst[:, par, 1, n:n + 1],
                                                   ALU.add, ALU.mult)
                last.then_inc(b_xh, 1)

            def batch_stats(b, par):
                pool.wait_ge(b_sm, b + 2)
                await_(pool, b_lgs, b - 2)
                await_(pool, b_on, b)
                await_(pool, b_on0, b)
                await_(pool, b_on1, b)
                pass_on(pool, s_pool)
                nc.gpsimd.tensor_scalar(st2[:, par, 1, :], sm2[:, 1, :], 1.0 / D, EPS, ALU.mult, ALU.add
                                        ).then_inc(b_arg, 1)
                nc.gpsimd.tensor_scalar(ost[:, par, 0, :], sm2[:, 0, TB:2 * TB], -0.5, 0.0, ALU.mult, ALU.add)
                pool.wait_ge(b_arg, b + 2)
                nc.gpsimd.tensor_tensor(ost[:, par, 1, :], ost[:, par, 1, :], mhalf[:, :], ALU.pow
                                        ).then_inc(b_ost, 1)
                pool.wait_ge(b_ost, b + 2)
                nc.gpsimd.tensor_tensor(ost[:, par, 2, :], ost[:, par, 0, :], ost[:, par, 1, :], ALU.mult
                                        ).then_inc(b_ost1, 1)
                nc.gpsimd.tensor_tensor(tst[:, par, 1, :], tst[:, par, 1, :], mhalf[:, :], ALU.pow
                                        ).then_inc(b_rst, 1)

            def step(b, par):
                if live(b + 1):
                    norm_x2(b + 1, 1 - par, 0)
                    norm_x2(b + 1, 1 - par, 1)
                batch_stats(b, par)

            norm_x2(0, 0, 0)
            norm_x2(0, 0, 1)
            batch_stats(-1, 1)
            for b in range(4):
                step(b, b % 2)
            with pool.Fori(2, NB // 2 - 1) as b_2:
                step(2 * b_2, 0)
                step(2 * b_2 + 1, 1)
            for b in range(NB - 2, NB + 1):
                step(b, b % 2)

            pool.wait_ge(b_exp, NB)
            for par in range(2):
                pool.wait_ge(b_store[par], 16 * NB // 2)
            nc.gpsimd.iota(iota_i, [[1, NB * K]], base=0, channel_multiplier=0).then_inc(c_iota, 1)
            nc.gpsimd.memset(ones[:, :], 1.0).then_inc(c_iota, 1)
            nc.gpsimd.memset(pooled_d[:, :, :], 0.0).then_inc(c_zero, 1)
            nc.gpsimd.memset(hid_d[:, :, :], 0.0).then_inc(c_zero, 1)
            pool.wait_ge(c_v, V_IDX)
            for s in range(4):
                pool.indirect_dma_start(
                    out=t_rows[:, s, :], out_offset=None, in_=rows,
                    in_offset=bass.IndirectOffsetOnAxis(ap=idx_i[:, s:s + 1], axis=0)).then_inc(c_gather, 16)
            pool.wait_ge(c_v, V_VAR)
            nc.gpsimd.tensor_scalar(rst4[:, :], mv4[:, :, 1], 1.0, EPS, ALU.mult, ALU.add).then_inc(c_pool, 1)
            pool.wait_ge(c_pool, 1)
            nc.gpsimd.tensor_tensor(rst4[:, :], rst4[:, :], mhalf[:, 0:4], ALU.pow).then_inc(c_pool, 1)
            pool.wait_ge(c_v, V_PICKED)
            nc.gpsimd.memset(earlier[:, :, :], 1.0).then_inc(c_iota, 1)
            pool.wait_ge(c_iota, 3)
            nc.gpsimd.affine_select(out=earlier[:, :, :], in_=earlier[:, :, :],
                                    compare_op=ALU.is_gt, fill=0.0, base=0,
                                    pattern=[[P, 4], [-1, 4 * P]], channel_multiplier=1).then_inc(c_iota, 1)
            pool.wait_ge(c_v, V_NEW)
            for s in range(4):
                pool.indirect_dma_start(
                    out=rows, out_offset=bass.IndirectOffsetOnAxis(ap=idx_w[:, s:s + 1], axis=0),
                    in_=new_rows[:, s, :], in_offset=None, bounds_check=S - 1, oob_is_err=False
                ).then_inc(c_scatter, 16)
            pool.wait_ge(c_scatter, 64)

        @block.tensor
        def _(pe):
            pe.wait_ge(s_ident, 2)
            pe.wait_ge(s_wload, 16 * 14)
            for n in range(6):
                if n >= 2:
                    pe.wait_ge(s_wcopy, n - 1)
                nc.tensor.transpose(bank[n % 2][:, 0:P], wraw[:, n, :], ident[:, :]).then_inc(s_wt, 1)
            mrow = tout[:, :, :, :].rearrange("p s t d -> p (s t d)")[:, 0:NBLK * N].rearrange(
                "p (b k) -> p b k", b=NBLK)
            for n in range(NBLK * NBLK):
                pe.wait_ge(s_wcopy, n + 5)
                nc.tensor.transpose(bank[n % 2][:, 0:P], mrow[:, n // NBLK, (n % NBLK) * P:(n % NBLK + 1) * P],
                                    ident[:, :]).then_inc(s_wt, 1)
            pe.wait_ge(s_wcopy, 15)
            pe.wait_ge(s_gcen, 1)
            nc.tensor.transpose(bank[1][:, 0:E], wraw[0:E, 7, :], ident[0:E, 0:E]).then_inc(s_wt, 1)

            def transpose_x(u, h):
                pe.wait_ge(a_xh, u + 1)
                await_(pe, a_xn, u - 1)
                for t in range(TU):
                    last = nc.tensor.transpose(bank[h][:, t * P:(t + 1) * P], xh[:, h, t * D:(t + 1) * D],
                                               ident[:, :])
                last.then_inc(a_tp, 1)

            def project(u, h):
                pe.wait_ge(a_xn, u + 1)
                for t in range(TU):
                    await_(pe, a_side, 4 * (u - 1) + t + 1)
                    nc.tensor.matmul(bank[2 + t][:, :], xnt[:, h, t * P:(t + 1) * P], w_lr,
                                     start=True, stop=True).then_inc(a_lr, 1)

            pe.wait_ge(s_wcopy, 17)
            transpose_x(0, 0)
            for b in range(2):
                transpose_x(2 * b + 1, 1)
                project(2 * b, 0)
                transpose_x(2 * b + 2, 0)
                project(2 * b + 1, 1)
            with pe.Fori(2, NB - 1, 1) as b:
                transpose_x(2 * b + 1, 1)
                project(2 * b, 0)
                transpose_x(2 * b + 2, 0)
                project(2 * b + 1, 1)
            transpose_x(2 * NB - 1, 1)
            project(2 * NB - 2, 0)
            project(2 * NB - 1, 1)

            bx, bg, be, bo, bl, blt = bank[0], bank[1:3], bank[3], bank[4], bank[6], bank[7]
            by = [bank[5], bank[1]]
            bxo = [bx, bo]

            def triangle(eb, par, h, resident):
                if h == 0:
                    pe.wait_ge(b_lr[par], 32 * (eb // 2) + 32)
                    if resident:
                        pe.wait_ge(b_res[par], (eb // (NBLK * CB) - 1) * (16 * CB // 2) + 16 * ((eb % CB) // 2) + 16)
                await_(pe, b_triout, 2 * eb + h)
                for q in range(TU):
                    dd = h * TU + q
                    d = (eb % CB) * TB + dd
                    o = be[:, q * P:(q + 1) * P]
                    for k in range(2):
                        nc.tensor.matmul(o, right_res[:, k, ds(d, 1), :].rearrange("k o j -> k (o j)"),
                                         lr[:, par, k, dd, :], start=(k == 0), stop=False)
                    last = nc.tensor.matmul(o, lr[:, par, 3, dd, :], lr[:, par, 2, dd, :], start=False, stop=True)
                last.then_inc(b_tri, 1)

            def transpose_x2(b, h):
                pe.wait_ge(b_xh, 2 * b + h + 1)
                if h == 0:
                    await_(pe, b_tt, 2 * (b - 1))
                else:
                    await_(pe, b_onw, 2 * b)
                for t in range(TU):
                    last = nc.tensor.transpose(bxo[h][:, t * P:(t + 1) * P], xh[:, h, t * D:(t + 1) * D],
                                               ident[:, :])
                last.then_inc(b_xtp, 1)

            def gate(b, h):
                pe.wait_ge(b_xn, 2 * b + h + 1)
                if h == 0:
                    await_(pe, b_t, 2 * b)
                else:
                    await_(pe, b_gated, 2 * b)
                nc.tensor.matmul(bg[h][:, :], w_og[:, :], xnt[:, h, :], start=True, stop=True).then_inc(b_gate, 1)

            def transpose_on(b, h):
                pe.wait_ge(b_on1 if h else b_on, b + 1)
                if h == 0:
                    pe.wait_ge(b_on0, b + 1)
                if h == 0:
                    pe.wait_ge(b_xn, 2 * b + 2)
                else:
                    pe.wait_ge(b_onw, 2 * b + 1)
                for t in range(TU):
                    last = nc.tensor.transpose(bo[:, t * P:(t + 1) * P], on[:, h, t * D:(t + 1) * D], ident[:, :])
                last.then_inc(b_otp, 1)

            def project_out(b, h):
                pe.wait_ge(b_gated, 2 * b + h + 1)
                if h == 0:
                    await_(pe, b_t, 2 * b - 1)
                for t in range(TU):
                    last = nc.tensor.matmul(by[h][:, t * D:(t + 1) * D], gated[:, h, t * P:(t + 1) * P], w_o[:, :],
                                            start=True, stop=True)
                last.then_inc(b_y, 1)

            def transpose_t(b, par, h):
                pe.wait_ge(b_t, 2 * b + h + 1)
                if h == 0:
                    pe.wait_ge(b_xn, 2 * NB if isinstance(b, int) and b == NB - 1 else 2 * b + 3)
                else:
                    pe.wait_ge(b_tt, 2 * b + 1)
                for t in range(TU):
                    last = nc.tensor.transpose(bx[:, t * P:(t + 1) * P], tout[:, par, h * TU + t, :], ident[:, :])
                last.then_inc(b_ttp, 1)

            def logits(b, h):
                pe.wait_ge(b_tt, 2 * b + h + 1)
                if h == 0:
                    await_(pe, b_lgs, b)
                for t in range(TU):
                    at = (h * TU + t) * E
                    last = nc.tensor.matmul(bl[:, at:at + E], tt[:, h, t * P:(t + 1) * P], g_c[:, :],
                                            start=True, stop=True)
                last.then_inc(b_logit, 1)

            def transpose_logits(b):
                pe.wait_ge(b_lgs, b + 1)
                await_(pe, b_exp, b)
                for h in range(2):
                    for q in range(2):
                        at = (2 * h + q) * P
                        last = nc.tensor.transpose(blt[:, at:at + P], lgs[:, h, 2 * q * E:(2 * q + 2) * E],
                                                   ident[:, :])
                last.then_inc(b_ltp, 1)

            def step(b, par, tri=False, resident=False):
                if live(b):
                    transpose_x2(b, 1)
                    gate(b, 0)
                if live(b - 2):
                    transpose_logits(b - 2)
                if live(b):
                    transpose_on(b, 0)
                if live(b - 1):
                    transpose_t(b - 1, 1 - par, 0)
                if tri:
                    triangle(b + CB + 1, 1 - par, 0, resident)
                if live(b):
                    gate(b, 1)
                    transpose_on(b, 1)
                if live(b - 1):
                    transpose_t(b - 1, 1 - par, 1)
                if live(b - 1):
                    logits(b - 1, 0)
                if live(b):
                    project_out(b, 0)
                if live(b + 1):
                    transpose_x2(b + 1, 0)
                if live(b):
                    project_out(b, 1)
                if live(b - 1):
                    logits(b - 1, 1)
                if tri:
                    triangle(b + CB + 1, 1 - par, 1, resident)

            pe.wait_ge(a_side, 8 * NB)
            pe.wait_ge(b_resfirst, 64)
            for eb in range(2):
                for h in range(2):
                    triangle(eb, eb, h, False)
            with pe.Fori(1, CB // 2) as eb_2:
                for par in range(2):
                    for h in range(2):
                        triangle(2 * eb_2 + par, par, h, False)
            for h in range(2):
                triangle(CB, 0, h, False)
            transpose_x2(0, 0)
            for b in range(3):
                step(b, b % 2, True)
            for lo, hi, tri_on, resident in [(3, 31, True, False), (31, 47, True, True), (47, 79, True, False),
                                             (79, 95, True, True), (95, NB - CB - 1, True, False),
                                             (NB - CB - 1, NB - 1, False, False)]:
                with pe.Fori((lo - 1) // 2, (hi - 1) // 2) as b_2:
                    for k in range(2):
                        step(2 * b_2 + 1 + k, 1 - k, tri_on, resident)
            for b in range(NB - 1, NB + 2):
                step(b, b % 2)

            pe.wait_ge(c_v, V_DIAG)
            pe.wait_ge(c_iota, 2)
            nc.tensor.matmul(bank[2][:, :], ones[0:E, 0:P], diag[0:E, :], start=True, stop=True).then_inc(c_row, 1)
            for s in range(4):
                pe.wait_ge(c_v, V_U + s)
                last = nc.tensor.matmul(bank[3][:, 0:E], u_rows[:, s, :], dtop[:, s, :], start=(s == 0), stop=(s == 3))
            last.then_inc(c_pooled, 1)
            pe.wait_ge(c_v, V_PT)

            for g in range(2):
                rows_g = slice(g * EG, (g + 1) * EG)
                for e in range(EG):
                    if e % XG == 0:
                        if g == 0:
                            pe.wait_ge(c_early, 3 * XG * 32)
                            if e == 3 * XG:
                                pe.wait_ge(c_w3, XG * 32)
                        else:
                            pe.wait_ge(c_w1[e // XG], XG * 16)
                    last = nc.tensor.matmul(bank[4][rows_g, :], pooled_d[:, g, e * EG:(e + 1) * EG],
                                            experts[:, e, 0, :], start=(e == 0), stop=(e == EG - 1))
                    if e % XG == XG - 1:
                        last.then_inc(c_l1, 1)
                pe.wait_ge(c_gelu, g + 1)
                for c in range(HC):
                    last = nc.tensor.transpose(bank[6][:, c * EG:(c + 1) * EG], hid[rows_g, c * P:(c + 1) * P],
                                               ident[rows_g, rows_g])
                last.then_inc(c_htp, 1)
                pe.wait_ge(c_hd, g + 1)
                for e in range(EG):
                    if g == 1 and e % XG == 0:
                        pe.wait_ge(c_w2[e // XG], XG * 16)
                    for c in range(HC):
                        last = nc.tensor.matmul(bank[5][rows_g, 0:D], hid_d[:, c, e * EG:(e + 1) * EG],
                                                experts[:, e, 1, c * P:(c + 1) * P],
                                                start=(e == 0 and c == 0), stop=(e == EG - 1 and c == HC - 1))
                    if e % XG == XG - 1:
                        last.then_inc(c_l2, 1)
            pe.wait_ge(c_v, V_OE)
            for s in range(4):
                last = nc.tensor.matmul(bank[7][:, s * D:(s + 1) * D], share[0:E, s * P:(s + 1) * P], out_e[0:E, :],
                                        start=True, stop=True)
            last.then_inc(c_delta, 1)

        @block.scalar
        def _(act):
            nw, nb_, ow, ob = (cols[:, n:n + 1] for n in range(4))

            def out_of_x(u, h):
                act.wait_ge(a_tp, u + 1)
                await_(act, a_lr, 4 * (u - 1))
                nc.scalar.activation(xnt[:, h, :], bank[h][:, :], ACT.Identity, bias=nb_, scale=nw
                                     ).then_inc(a_xn, 1)

            def sigmoids(u, h):
                for j in range(2):
                    for t in range(2):
                        act.wait_ge(a_lr, 4 * u + 2 * j + t + 1)
                        await_(act, a_side, 4 * (u - 1) + 2 * j + t + 1)
                        nc.scalar.activation(sig[:, j, t, :], bank[2 + 2 * j + t][:, 2 * D:4 * D], ACT.Sigmoid
                                             ).then_inc(a_sig, 1)

            act.wait_ge(s_wload, 16 * 14)
            act.wait_ge(s_wcopy, 17)
            out_of_x(0, 0)
            for b in range(2):
                out_of_x(2 * b + 1, 1)
                sigmoids(2 * b, 0)
                out_of_x(2 * b + 2, 0)
                sigmoids(2 * b + 1, 1)
            with act.Fori(2, NB - 1, 1) as b:
                out_of_x(2 * b + 1, 1)
                sigmoids(2 * b, 0)
                out_of_x(2 * b + 2, 0)
                sigmoids(2 * b + 1, 1)
            out_of_x(2 * NB - 1, 1)
            sigmoids(2 * NB - 2, 0)
            sigmoids(2 * NB - 1, 1)

            bx, bg, be, bo, blt = bank[0], bank[1:3], bank[3], bank[4], bank[7]
            bxo = [bx, bo]

            def out_of_triangle(eb, h, reused):
                act.wait_ge(b_tri, 2 * eb + h + 1)
                if reused:
                    act.wait_ge(b_on, CB * ((eb - CB) // CB))
                    act.wait_ge(b_on1, CB * ((eb - CB) // CB))
                nc.scalar.activation(
                    tri[:, ds((eb // CB + 1) % 2, 1), :, ds((eb % CB) * TB + h * TU, TU)].rearrange(
                        "j o i d -> j (o i) d"),
                    be[:, :].rearrange("j (d i) -> j i d", d=TU), ACT.Copy).then_inc(b_triout, 1)

            def norm_o1(b, par, h):
                if h == 0:
                    act.wait_ge(b_ost1, b + 1)
                await_(act, b_otp, 2 * (b - 1) + h + 1)
                for t in range(TU) if h else range(DVE_TILES, TU):
                    n = h * TU + t
                    last = nc.scalar.activation(
                        on[:, h, t * D:(t + 1) * D],
                        tri[:, ds((b // CB + 1) % 2, 1), ds((b % CB) * TB + n, 1), :].rearrange(
                            "j o i d -> j (o i d)"),
                        ACT.Identity, bias=ost[:, 1 - par, 2, n:n + 1], scale=ost[:, 1 - par, 1, n:n + 1])
                last.then_inc(b_on1 if h else b_on0, 1)

            def out_of_x2(b, h):
                act.wait_ge(b_xtp, 2 * b + h + 1)
                await_(act, b_gate, 2 * (b - 1) + h + 1)
                nc.scalar.activation(xnt[:, h, :], bxo[h][:, :], ACT.Identity, bias=nb_, scale=nw).then_inc(b_xn, 1)

            def gate_tanh(b, h):
                act.wait_ge(b_gate, 2 * b + h + 1)
                nc.scalar.activation(bg[h][:, :], bg[h][:, :], ACT.Tanh, scale=0.5).then_inc(b_tanh, 1)

            def out_of_on(b, h):
                act.wait_ge(b_otp, 2 * b + h + 1)
                await_(act, b_y, 2 * (b - 1) + h + 1)
                nc.scalar.activation(gated[:, h, :], bo[:, :], ACT.Identity, bias=ob, scale=ow).then_inc(b_onw, 1)

            def out_of_t(b, h):
                act.wait_ge(b_ttp, 2 * b + h + 1)
                await_(act, b_logit, 2 * (b - 1) + h + 1)
                nc.scalar.activation(tt[:, h, :], bx[:, :], ACT.Copy).then_inc(b_tt, 1)

            def exps(b):
                act.wait_ge(b_negm, b + 1)
                nc.scalar.activation(blt[:, :], blt[:, :], ACT.Exp, bias=negm[:, :],
                                     accum_out=csum[:, ds(b, 1)]).then_inc(b_exp, 1)

            def step(b, par, tri_on=False, reused=False):
                if live(b):
                    out_of_x2(b, 1)
                    gate_tanh(b, 0)
                    out_of_on(b, 0)
                if live(b - 1):
                    out_of_t(b - 1, 0)
                if tri_on:
                    out_of_triangle(b + CB + 1, 0, reused)
                if live(b):
                    gate_tanh(b, 1)
                    out_of_on(b, 1)
                if live(b - 1):
                    out_of_t(b - 1, 1)
                if live(b + 1):
                    norm_o1(b + 1, 1 - par, 0)
                    out_of_x2(b + 1, 0)
                    norm_o1(b + 1, 1 - par, 1)
                if tri_on:
                    out_of_triangle(b + CB + 1, 1, reused)
                if live(b - 2):
                    exps(b - 2)

            nc.scalar.activation(csum[:, 0:1], mhalf[:, 0:1], ACT.Exp)
            act.wait_ge(a_last[1], 64)
            with act.Fori(0, CB, 1) as eb0:
                for h in range(2):
                    act.wait_ge(b_tri, 2 * eb0 + h + 1)
                    nc.scalar.activation(tri[:, 1, :, ds(eb0 * TB + h * TU, TU)],
                                         be[:, :].rearrange("j (d i) -> j i d", d=TU), ACT.Copy
                                         ).then_inc(b_triout, 1)
            act.wait_ge(a_last[0], 64)
            for h in range(2):
                out_of_triangle(CB, h, False)
            out_of_x2(0, 0)
            norm_o1(0, 0, 0)
            norm_o1(0, 0, 1)
            for b in range(3):
                step(b, b % 2, True)
            for lo, hi, tri_on, reused in [(3, CB - 1, True, False), (CB - 1, NB - CB - 1, True, True),
                                           (NB - CB - 1, NB - 1, False, False)]:
                with act.Fori((lo - 1) // 2, (hi - 1) // 2) as b_2:
                    for k in range(2):
                        step(2 * b_2 + 1 + k, 1 - k, tri_on, reused)
            for b in range(NB - 1, NB + 2):
                step(b, b % 2)

            act.wait_ge(c_v, V_TOP)
            nc.scalar.activation(wexp[:, :], cand[:, :, 0], ACT.Exp, bias=negtop[:, :]).then_inc(c_act, 1)
            act.wait_ge(c_v, V_M2)
            nc.scalar.activation(hm[0:E, :], both[0:E, :, 16], ACT.Exp, bias=neg2[0:E, :]).then_inc(c_act, 1)
            nc.scalar.activation(ev[0:E, :], v8[0:E, :], ACT.Exp, bias=neg2[0:E, :]).then_inc(c_act, 1)

            for g in range(2):
                act.wait_ge(c_hb, g + 1)
                nc.scalar.activation(hid[g * EG:(g + 1) * EG, :], hpre[g * EG:(g + 1) * EG, :], ACT.Gelu
                                     ).then_inc(c_gelu, 1)

        @block.vector
        def _(dve):
            dests = [w_lr[:, n * D:(n + 1) * D] for n in range(4)] + [w_og[:, :]]
            for n in range(15):
                dve.wait_ge(s_wt, n + 1)
                src = bank[n % 2][:, 0:P]
                if n < 5:
                    nc.vector.tensor_copy(dests[n], src).then_inc(s_wcopy, 1)
                elif n == 5:
                    nc.vector.tensor_scalar(w_o[:, :], src, 0.5, None, ALU.mult).then_inc(s_wcopy, 1)
                else:
                    m = n - 6
                    nc.vector.tensor_copy(mask_t[:, m % NBLK, (m // NBLK) * P:(m // NBLK + 1) * P], src
                                          ).then_inc(s_wcopy, 1)
                if n == 5:
                    nc.vector.reduce_sum(negm[0:E, :], wraw[0:E, 6, :], axis=AX.X).then_inc(s_gmean, 1)
                    dve.wait_ge(s_gmean, 1)
                    nc.vector.tensor_scalar(tmp[0:E, 0, 0:1], negm[0:E, :], 1.0 / D, None, ALU.mult
                                            ).then_inc(s_gmean, 1)
                    dve.wait_ge(s_gmean, 2)
                    nc.vector.tensor_scalar(wraw[0:E, 7, :], wraw[0:E, 6, :], tmp[0:E, 0, 0:1], None,
                                            ALU.subtract).then_inc(s_gcen, 1)
            dve.wait_ge(s_wt, 16)
            nc.vector.tensor_copy(g_c[:, :], bank[1][:, 0:E]).then_inc(s_wcopy, 2)

            def moments(n, count, dst, s_1, s_2, s_out):
                nc.vector.tensor_tensor(tmp[:, 0, 0:n], bst[:, 0:n, 1], bst[:, 0:n, 4], ALU.subtract
                                        ).then_inc(s_1, 1)
                nc.vector.tensor_tensor(dst[:, 0, :], bst[:, 0:n, 1], bst[:, 0:n, 4], ALU.add)
                nc.vector.tensor_tensor(tmp[:, 1, 0:n], bst[:, 0:n, 2], bst[:, 0:n, 5], ALU.add)
                dve.wait_ge(s_1, count)
                nc.vector.scalar_tensor_tensor(tmp[:, 2, 0:n], tmp[:, 0, 0:n], D / 4.0, tmp[:, 0, 0:n],
                                               ALU.mult, ALU.mult).then_inc(s_2, 1)
                dve.wait_ge(s_2, count)
                nc.vector.tensor_tensor(dst[:, 1, :], tmp[:, 1, 0:n], tmp[:, 2, 0:n], ALU.add).then_inc(s_out, 1)

            def tile_stats(b, slot, t):
                if t == 0:
                    dve.wait_ge(a_x[slot], 16 * (b // 4) + 16)
                last = nc.vector.bn_stats(bst[:, t, :], x_slots[slot][:, t, :])
                if t == TB - 1:
                    last.then_inc(a_bn, 1)

            def end_stats(b, slot):
                await_(dve, a_pow, b - 1)
                dve.wait_ge(a_bn, b + 1)
                moments(TB, b + 1, sm[:, slot % 2, :, :], a_s1, a_s2, a_sm)

            def stage_sides(b, stored, stats_too=None):
                if stored:
                    dve.wait_ge(a_store, 8 * 16 * ((b - CB) // CB))
                c = b // CB
                for n in range(TB):
                    dve.wait_ge(a_sig, TB * b + n + 1)
                    i = (b % RB) * TB + n
                    il = (b % CB) * TB + n
                    nc.vector.scalar_tensor_tensor(
                        stage[:, ds((c + 1) % 2, 1), :, :, ds(il, 1)].rearrange("k o s d i -> k (o s) (d i)"),
                        bank[2 + n % 4][:, 0:2 * D].rearrange("k (s d) -> k s d", s=2),
                        mask_t[:, ds(b // RB, 1), ds(i, 1)].rearrange("k o i -> k (o i)"),
                        sig[:, (n // 2) % 2, n % 2, :].rearrange("k (s d) -> k s d", s=2),
                        ALU.mult, ALU.mult).then_inc(a_side, 1)
                    if stats_too is not None:
                        tile_stats(b + 3, stats_too, n)
                if stats_too is not None:
                    end_stats(b + 3, stats_too)

            dve.wait_ge(s_wcopy, 17)
            nc.vector.memset(bst[:, :, :], 0.0).then_inc(s_dve, 1)
            dve.wait_ge(s_dve, 1)
            for b in range(3):
                for t in range(TB):
                    tile_stats(b, b, t)
                end_stats(b, b)
            for b in range(4):
                stage_sides(b, False, (b + 3) % 4)
            for lo, hi, stored in [(4, 2 * CB, False), (2 * CB, NB - 4, True)]:
                with dve.Fori(lo // 4, hi // 4) as q:
                    for k in range(4):
                        stage_sides(4 * q + k, stored, (k + 3) % 4)
            for b in range(NB - 4, NB):
                stage_sides(b, True, (b + 3) % 4 if b + 3 < NB else None)

            bg, by, bl, blt = bank[1:3], [bank[5], bank[1]], bank[6], bank[7]

            def take_maxima(b):
                dve.wait_ge(b_ltp, b + 1)
                pass_on(dve, s_dve)
                nc.vector.max(m8[:, :], blt[:, :]).then_inc(b_m8, 1)

            def keep_maxima(b):
                dve.wait_ge(b_m8, b + 1)
                nc.vector.tensor_copy(cand[:, ds(b, 1), :], m8[:, :].rearrange("p (o k) -> p o k", o=1))

            def find_maxima(b):
                nc.vector.max_index(i8[:, :], m8[:, :], blt[:, :]).then_inc(b_i8, 1)
                await_(dve, b_exp, b)
                nc.vector.tensor_scalar(negm[:, :], m8[:, 0:1], -1.0, None, ALU.mult).then_inc(b_negm, 1)

            def keep_index(b):
                dve.wait_ge(b_i8, b + 1)
                nc.vector.tensor_copy(cidx[:, ds(b, 1), :], i8[:, :].rearrange("p (o k) -> p o k", o=1)
                                      ).then_inc(b_keep, 1)

            def batch_stats(b, par):
                if live(b + 1):
                    dve.wait_ge(b_triout, 2 * CB * ((b + 1) // CB) + 2 * CB)
                    for t in range(TB):
                        last = nc.vector.bn_stats(bst[:, TB + t, :], tri_tile(b + 1, t))
                if live(b - 1):
                    dve.wait_ge(b_t, 2 * b)
                    for t in range(TB):
                        last = nc.vector.bn_stats(bst[:, t, :], tout[:, 1 - par, t, :])
                last.then_inc(b_bn, 1)
                if live(b - 2):
                    take_maxima(b - 2)
                dve.wait_ge(b_bn, b + 2)
                nc.vector.tensor_tensor(tmp[:, 0, :], bst[:, :, 1], bst[:, :, 4], ALU.subtract).then_inc(b_s1, 1)
                nc.vector.tensor_tensor(sm2[:, 0, :], bst[:, :, 1], bst[:, :, 4], ALU.add)
                nc.vector.tensor_tensor(tmp[:, 1, :], bst[:, :, 2], bst[:, :, 5], ALU.add)
                dve.wait_ge(b_s1, b + 2)
                nc.vector.scalar_tensor_tensor(tmp[:, 2, :], tmp[:, 0, :], D / 4.0, tmp[:, 0, :],
                                               ALU.mult, ALU.mult).then_inc(b_s2, 1)
                if live(b - 2):
                    keep_maxima(b - 2)
                dve.wait_ge(b_s2, b + 2)
                nc.vector.tensor_tensor(sm2[:, 1, :], tmp[:, 1, :], tmp[:, 2, :], ALU.add).then_inc(b_sm, 1)

            def gates(b, h):
                dve.wait_ge(b_tanh, 2 * b + h + 1)
                dve.wait_ge(b_onw, 2 * b + h + 1)
                nc.vector.scalar_tensor_tensor(gated[:, h, :], bg[h][:, :], 1.0, gated[:, h, :], ALU.add, ALU.mult
                                               ).then_inc(b_gated, 1)

            def scale_logits(b, par):
                dve.wait_ge(b_logit, 2 * b + 2)
                dve.wait_ge(b_rst, b + 3)
                await_(dve, b_ltp, b)
                nc.vector.tensor_tensor(
                    lgs[:, :, :].rearrange("p h (t e) -> p (h t) e", t=TU),
                    bl[:, :].rearrange("p (t e) -> p t e", t=TB),
                    tst[:, 1 - par, 1, :].unsqueeze(2).broadcast_to([P, TB, E]), ALU.mult
                ).then_inc(b_lgs, 1)

            def residual(b, par, h):
                dve.wait_ge(b_y, 2 * b + h + 1)
                if h == 0:
                    await_(dve, b_store[par], 16 * (b // 2))
                await_(dve, b_ttp, 2 * (b - 2) + h + 1)
                nc.vector.tensor_tensor(tout[:, par, h * TU:(h + 1) * TU, :],
                                        by[h][:, :].rearrange("p (t d) -> p t d", t=TU),
                                        xin[:, par, h * TU:(h + 1) * TU, :], ALU.add).then_inc(b_t, 1)

            def tri_tile(b, t):
                return tri[:, ds((b // CB + 1) % 2, 1), ds((b % CB) * TB + t, 1), :].rearrange("j o i d -> j (o i d)")

            def norm_o(b, par):
                dve.wait_ge(b_ost, b + 1)
                await_(dve, b_otp, 2 * (b - 1) + 1)
                for t in range(DVE_TILES):
                    last = nc.vector.tensor_scalar(on[:, 0, t * D:(t + 1) * D], tri_tile(b, t),
                                                   ost[:, 1 - par, 0, t:t + 1],
                                                   ost[:, 1 - par, 1, t:t + 1], ALU.add, ALU.mult)
                last.then_inc(b_on, 1)

            def step(b, par):
                if live(b - 1) or live(b + 1):
                    batch_stats(b, par)
                elif live(b - 2):
                    take_maxima(b - 2)
                    keep_maxima(b - 2)
                if live(b - 2):
                    find_maxima(b - 2)
                if live(b):
                    gates(b, 0)
                if live(b - 2):
                    keep_index(b - 2)
                if live(b):
                    gates(b, 1)
                if live(b):
                    residual(b, par, 0)
                if live(b + 1):
                    norm_o(b + 1, 1 - par)
                if live(b):
                    residual(b, par, 1)
                if live(b - 1):
                    scale_logits(b - 1, 1 - par)

            batch_stats(-1, 1)
            norm_o(0, 0)
            for b in range(4):
                step(b, b % 2)
            with dve.Fori(2, NB // 2 - 1) as b_2:
                step(2 * b_2, 0)
                step(2 * b_2 + 1, 1)
            for b in range(NB - 2, NB + 2):
                step(b, b % 2)

            count = [0]

            def done(ins):
                count[0] += 1
                ins.then_inc(c_v, 1)
                dve.wait_ge(c_v, count[0])

            def mark(value):
                assert count[0] == value, (count[0], value)

            dve.wait_ge(b_exp, NB)
            for par in range(2):
                dve.wait_ge(b_store[par], 16 * NB // 2)
            dve.wait_ge(b_keep, NB)
            cflat = cand[:, :, :].rearrange("p b k -> p (b k)")
            iflat = cidx[:, :, :].rearrange("p b k -> p (b k)")
            done(nc.vector.memset(par384[0:E, :], 0.0))
            done(nc.vector.memset(par384[E:2 * E, :], float(N)))
            done(nc.vector.tensor_scalar(cflat, cflat, gb[:, :], None, ALU.add))
            done(nc.vector.max(both[:, 0, 0:8], cflat))
            done(nc.vector.tensor_scalar(negtop[:, :], both[:, 0, 0:1], -1.0, None, ALU.mult))
            mark(V_TOP)
            done(nc.vector.max_index(pos_i[:, :], both[:, 0, 0:8], cflat))
            done(nc.vector.tensor_copy(pos_f[:, :], pos_i[:, :]))
            dve.wait_ge(c_iota, 1)
            done(nc.vector.tensor_copy(iota_f, iota_i))
            for k in range(K):
                last = nc.vector.scalar_tensor_tensor(pick, iota_f, pos_f[:, k:k + 1], iflat, ALU.is_equal, ALU.mult,
                                                      accum_out=raw[:, k:k + 1])
                if k < K - 1:
                    done(last)
            done(last)
            done(nc.vector.tensor_copy(raw_i[:, :], raw[:, :]))
            done(nc.vector.tensor_scalar(bi[:, :], pos_i[:, :], 3, None, ALU.logical_shift_right))
            done(nc.vector.tensor_scalar(qi[:, :], raw_i[:, :], 7, None, ALU.logical_shift_right))
            done(nc.vector.tensor_copy(bf[:, :], bi[:, :]))
            done(nc.vector.tensor_copy(qf[:, :], qi[:, :]))
            done(nc.vector.scalar_tensor_tensor(tok[:, :], qf[:, :], float(2 * N - P), raw[:, :], ALU.mult, ALU.add))
            done(nc.vector.scalar_tensor_tensor(tok[:, :], bf[:, :], float(TB * N), tok[:, :], ALU.mult, ALU.add))
            dve.wait_ge(c_iota, 2)
            done(nc.vector.tensor_scalar(tok[:, :], tok[:, :], par384[:, :], None, ALU.add))
            for m in range(1, NBLK):
                done(nc.vector.tensor_scalar(qf[:, :], bf[:, :], float(m * RB), float(P - S), ALU.is_ge, ALU.mult))
                done(nc.vector.tensor_tensor(both[:, 0, 8:16] if m == NBLK - 1 else tok[:, :], tok[:, :], qf[:, :],
                                             ALU.add))
            done(nc.vector.tensor_copy(both[:, 0, 16:17], both[:, 0, 0:1]))
            dve.wait_ge(c_act, 1)
            done(nc.vector.tensor_tensor(wexp[:, :], wexp[:, :], csum[:, :], ALU.mult))
            done(nc.vector.reduce_sum(both[:, 0, 17:18], wexp[:, :], axis=AX.X))
            mark(V_FIN)
            dve.wait_ge(c_half, 16)
            done(nc.vector.tensor_copy(v16[0:E, :, :], both[0:E, :, 0:8]))
            done(nc.vector.tensor_copy(t16[0:E, :, :], both[0:E, :, 8:16]))
            v16f = v16[0:E, :, :].rearrange("p s k -> p (s k)")
            t16f = t16[0:E, :, :].rearrange("p s k -> p (s k)")
            done(nc.vector.max(v8[0:E, :], v16f))
            done(nc.vector.tensor_scalar(neg2[0:E, :], v8[0:E, 0:1], -1.0, None, ALU.mult))
            mark(V_M2)
            done(nc.vector.max_index(pos_i[0:E, :], v8[0:E, :], v16f))
            done(nc.vector.tensor_copy(pos_f[0:E, :], pos_i[0:E, :]))
            for k in range(K):
                done(nc.vector.scalar_tensor_tensor(pick[0:E, 0:16], iota_f[0:E, 0:16], pos_f[0:E, k:k + 1], t16f,
                                                    ALU.is_equal, ALU.mult, accum_out=kv[0:E, 0, k:k + 1]))
            dve.wait_ge(c_act, 3)
            done(nc.vector.tensor_tensor(hm[0:E, :], hm[0:E, :], both[0:E, :, 17], ALU.mult))
            done(nc.vector.reduce_sum(den[0:E, :], hm[0:E, :], axis=AX.X))
            done(nc.vector.reciprocal(den[0:E, :], den[0:E, :]))
            done(nc.vector.tensor_scalar(kv[0:E, 1, :], ev[0:E, :], den[0:E, :], None, ALU.mult))
            mark(V_KV)
            done(nc.vector.tensor_tensor(
                diag[0:E, :].rearrange("p (k e) -> p k e", k=K),
                ident[0:E, 0:E].unsqueeze(1).broadcast_to([E, K, E]),
                kv[0:E, 0, :].unsqueeze(2).broadcast_to([E, K, E]), ALU.mult))
            mark(V_DIAG)
            dve.wait_ge(c_kv, 16)
            for half in range(2):
                sl = slice(half * E, (half + 1) * E)
                done(nc.vector.tensor_copy(sel[sl, :, :],
                                           kv[sl, :, :].rearrange("p v (s h) -> p v s h", h=2)[:, :, :, half]))
            done(nc.vector.tensor_copy(idx_i[:, :], sel[:, 0, :]))
            mark(V_IDX)
            dve.wait_ge(c_row, 1)
            done(nc.vector.tensor_copy(idx_row[:, :], bank[2][:, :]))
            done(nc.vector.tensor_scalar(share[0:E, :], idx_row[0:E, :], kv[0:E, 0, 0:1], kv[0:E, 1, 0:1],
                                         ALU.is_equal, ALU.mult))
            for k in range(1, K):
                done(nc.vector.tensor_scalar(part[0:E, :], idx_row[0:E, :], kv[0:E, 0, k:k + 1], kv[0:E, 1, k:k + 1],
                                             ALU.is_equal, ALU.mult))
                done(nc.vector.tensor_tensor(share[0:E, :], share[0:E, :], part[0:E, :], ALU.add))
            done(nc.vector.tensor_copy(id2[0:E, :], ident[0:E, 0:E]))
            done(nc.vector.tensor_copy(id2[E:2 * E, :], ident[E:2 * E, E:2 * E]))
            for s in range(4):
                done(nc.vector.tensor_scalar(dtop[:, s, :], id2[:, :], sel[:, 1, s:s + 1], None, ALU.mult))
            dve.wait_ge(c_gather, 64)
            for s in range(4):
                done(nc.vector.bn_stats(bst[:, s, :], t_rows[:, s, :]))
            for s in range(4):
                done(nc.vector.bn_aggr(mv4[:, s, :], bst[:, s, :]))
            mark(V_VAR)
            dve.wait_ge(c_pool, 2)
            for s in range(4):
                done(nc.vector.tensor_scalar(u_rows[:, s, :], t_rows[:, s, :], mv4[:, s, 0:1], rst4[:, s:s + 1],
                                             ALU.subtract, ALU.mult))
                mark(V_U + s)
            dve.wait_ge(c_pooled, 1)
            dve.wait_ge(c_zero, 2)
            for g in range(2):
                done(nc.vector.tensor_copy(pooled_d[:, g, 0:EG * EG:EG + 1], bank[3][:, g * EG:(g + 1) * EG]))
            mark(V_PT)
            dve.wait_ge(c_iota, 4)
            for s in range(4):
                done(nc.vector.scalar_tensor_tensor(part[:, :], idx_row[:, :], sel[:, 0, s:s + 1], earlier[:, s, :],
                                                    ALU.is_equal, ALU.mult, accum_out=dup[:, s:s + 1]))
            done(nc.vector.scalar_tensor_tensor(dup[:, :], dup[:, :], float(S), sel[:, 0, :], ALU.mult, ALU.add))
            done(nc.vector.tensor_copy(idx_w[:, :], dup[:, :]))

            dve.wait_ge(c_bias, 32)
            for g in range(2):
                rows_g = slice(g * EG, (g + 1) * EG)
                dve.wait_ge(c_l1, 4 * g + 4)
                nc.vector.tensor_tensor(hpre[rows_g, :], bank[4][rows_g, :], b1_rows[rows_g, :], ALU.add
                                        ).then_inc(c_hb, 1)
                dve.wait_ge(c_htp, g + 1)
                await_(dve, c_l2, 4 * g)
                nc.vector.tensor_copy(hid_d[:, :, 0:EG * EG:EG + 1],
                                      bank[6][:, 0:HC * EG].rearrange("p (c e) -> p c e", c=HC)).then_inc(c_hd, 1)
            dve.wait_ge(c_l2, 8)
            done(nc.vector.tensor_tensor(out_e[0:E, :], bank[5][0:E, 0:D], b2_rows[0:E, :], ALU.add))
            mark(V_OE)
            dve.wait_ge(c_delta, 1)
            done(nc.vector.tensor_tensor(new_rows[:, :, :], bank[7][:, :].rearrange("p (s d) -> p s d", s=4),
                                         t_rows[:, :, :], ALU.add))
            mark(V_NEW)


_INS = ['x', 'L0_conv_mask', 'L0_conv_norm_w', 'L0_conv_norm_b', 'L0_conv_W_left', 'L0_conv_W_right',
        'L0_conv_W_left_gate', 'L0_conv_W_right_gate', 'L0_conv_W_out_gate', 'L0_conv_out_norm_w',
        'L0_conv_out_norm_b', 'L0_conv_W_out', 'L0_ffn_gate_w', 'L0_ffn_gate_b', 'L0_ffn_weight1',
        'L0_ffn_weight2']


def kernel(**inputs):
    import numpy as _np
    import concourse.bacc as _bacc
    from concourse import mybir as _mybir
    from concourse.bass_utils import run_bass_kernel_spmd as _run

    nc = _bacc.Bacc("TRN2", target_bir_lowering=False, num_devices=1)
    arrays, args = {}, []
    for name in _INS:
        a = _np.ascontiguousarray(inputs[name])
        arrays[f"in_{name}_dram"] = a
        args.append(nc.dram_tensor(f"in_{name}_dram", a.shape, _mybir.dt.from_np(a.dtype), kind="ExternalInput").ap())
    shape = inputs["x"].shape
    args.append(nc.dram_tensor("out_0_dram", shape, _mybir.dt.float32, kind="ExternalOutput").ap())
    metaformer_layer_kernel(nc, *args)
    r = _run(nc, [arrays], core_ids=[0])
    return r.results[0]["out_0_dram"]
```
